# Optimizing a Trainium2 kernel written in Bass

```python
import numpy as np
import jax
import jax.numpy as jnp

def _softmax(x, axis=-1):
    return jax.nn.softmax(x, axis=axis)

def _gelu(x):
    return jax.nn.gelu(x, approximate=True)

def _silu(x):
    return jax.nn.silu(x)

def _sigmoid(x):
    return jax.nn.sigmoid(x)

def _layernorm(x, axis=-1, eps=1e-05):
    m = jnp.mean(x, axis=axis, keepdims=True)
    v = jnp.var(x, axis=axis, keepdims=True)
    return (x - m) / jnp.sqrt(v + eps)

def _scatter_add(tgt, idx, src, axis=0):
    return tgt.at[idx].add(src)

def _segment_sum(src, seg, n):
    return jax.ops.segment_sum(src, seg, n)
kernel_name = 'mk_adj_resnorm_d2_adj_r2_7188f0'

def setup_inputs(seed: int=0):
    np.random.seed(seed)
    _w = jnp.asarray

    def _rec_inputs():
        import jax
        import jax.numpy as jnp
        _gk = jax.random.key(seed)
        x = -0.0002037 + 1 * jax.random.normal(jax.random.fold_in(_gk, 1), (5000, 128), jnp.float32)
        _a = jax.random.bernoulli(jax.random.fold_in(_gk, 2), 0.0032, (5000, 5000))
        _a = jnp.logical_or(_a, jnp.swapaxes(_a, -1, -2))
        _a = jnp.logical_or(_a, jnp.eye(5000, dtype=bool))
        _af = _a.astype(jnp.float32)
        adj = _af
        return (x, adj)
    x, adj = _rec_inputs()

    def _L0_gnn_setup():
        import jax, jax.numpy as jnp
        import numpy as np
        N = 5000
        F = 128
        C = 16
        AL = 0.1
        EPS = 1e-12
        key = jax.random.key(seed)
        k1, k2, k3, k4 = jax.random.split(key, 4)
        A = (jax.random.uniform(k1, (N, N)) > 0.99).astype(jnp.float32)
        x = jax.random.normal(k2, (N, F), dtype=jnp.float32)
        h0 = jax.random.normal(k3, (N, F), dtype=jnp.float32)
        labels = jax.random.randint(k4, (N,), 0, C)
        y = jax.nn.one_hot(labels, C, dtype=jnp.float32)
        return {'input': x, 'A': A, 'h0': h0, 'y': y}
    _L0_gnn_all = _L0_gnn_setup()
    _L0_gnn_in = {k: v for k, v in _L0_gnn_all.items() if k in ('h0', 'y')}
    del _L0_gnn_all

    def _L1_gnn_setup():
        import jax, jax.numpy as jnp
        import numpy as np
        N = 3072
        HID = 128
        T = 350
        DENSITY = 0.05
        key = jax.random.key(seed)
        k1, k2, k3, k4, k5, k6 = jax.random.split(key, 6)
        h = jax.random.normal(k1, (N, HID), dtype=jnp.float32)
        a = jax.random.uniform(k2, (N, N), dtype=jnp.float32)
        mask = jax.random.uniform(k3, (N, N)) < DENSITY
        adj = jnp.where(mask, a, 0.0)
        simlar = jax.random.normal(k4, (N, N), dtype=jnp.float32)
        s = 1.0 / np.sqrt(HID)
        W_proj = jax.random.uniform(k5, (HID, HID), minval=-s, maxval=s, dtype=jnp.float32)
        b_proj = jnp.zeros((HID,), dtype=jnp.float32)
        W_gcn = jax.random.uniform(k6, (HID, HID), minval=-s, maxval=s, dtype=jnp.float32)
        b_gcn = jnp.zeros((HID,), dtype=jnp.float32)
        return {'h': h, 'adj': adj, 'simlar': simlar, 'W_proj': W_proj, 'b_proj': b_proj, 'W_gcn': W_gcn, 'b_gcn': b_gcn}
    _L1_gnn_all = _L1_gnn_setup()
    _L1_gnn_in = {k: v for k, v in _L1_gnn_all.items() if k in ('W_proj', 'b_proj', 'W_gcn', 'b_gcn')}
    del _L1_gnn_all
    return {'x': x, 'adj': adj, 'L0_gnn_h0': _L0_gnn_in['h0'], 'L0_gnn_y': _L0_gnn_in['y'], 'L1_gnn_W_proj': _L1_gnn_in['W_proj'], 'L1_gnn_b_proj': _L1_gnn_in['b_proj'], 'L1_gnn_W_gcn': _L1_gnn_in['W_gcn'], 'L1_gnn_b_gcn': _L1_gnn_in['b_gcn']}

def reference(x, adj, L0_gnn_h0, L0_gnn_y, L1_gnn_W_proj, L1_gnn_b_proj, L1_gnn_W_gcn, L1_gnn_b_gcn):
    import jax
    import jax.numpy as jnp

    def _L0_gnn_ref(input, A, h0, y):
        import jax, jax.numpy as jnp
        import numpy as np
        N = 5000
        F = 128
        C = 16
        AL = 0.1
        EPS = 1e-12
        adj = A * (y @ y.T)
        row_l1 = jnp.maximum(jnp.sum(jnp.abs(adj), axis=1, keepdims=True), EPS)
        adj = adj / row_l1
        support = adj @ input
        return (1.0 - AL) * support + AL * h0

    def _L1_gnn_ref(h, adj, simlar, W_proj, b_proj, W_gcn, b_gcn):
        import jax, jax.numpy as jnp
        import numpy as np
        N = 3072
        HID = 128
        T = 350
        DENSITY = 0.05
        sim = jnp.tanh(adj * simlar)
        filt = sim * (adj > 0).astype(sim.dtype)
        vals, idx = jax.lax.top_k(filt, T)
        nnz = jnp.sum(filt != 0, axis=1)
        keep = jnp.arange(T)[None, :] < nnz[:, None]
        rows = jnp.arange(filt.shape[0])[:, None]
        new_adj = jnp.zeros_like(filt).at[rows, idx].set(jnp.where(keep, vals, 0.0))
        h2 = jnp.tanh(h @ W_proj + b_proj)
        feat = jax.nn.relu(new_adj @ (h2 @ W_gcn) + b_gcn)
        return feat
    x = _layernorm(x + _L0_gnn_ref(x, adj, L0_gnn_h0, L0_gnn_y), axis=-1)
    x = _layernorm(x + _L1_gnn_ref(x, adj, adj, L1_gnn_W_proj, L1_gnn_b_proj, L1_gnn_W_gcn, L1_gnn_b_gcn), axis=-1)
    return x

_drawn_inputs = setup_inputs


def setup_inputs(seed=0):
    import zlib

    import numpy as np

    out = dict(_drawn_inputs(seed))
    spreads = {'L1_gnn_b_proj': (0.0, 0.1), 'L1_gnn_b_gcn': (0.0, 0.1)}
    factors = {}
    for name, (base, spread) in spreads.items():
        noise = np.random.default_rng([zlib.crc32(name.encode()), seed]).standard_normal(out[name].shape)
        drawn = base * np.exp(spread * noise) if base else spread * noise
        out[name] = jnp.asarray(drawn.astype(out[name].dtype))
    for name, factor in factors.items():
        out[name] = (out[name] * factor).astype(out[name].dtype)
    return out
```

```python
from contextlib import ExitStack

import concourse.bass as bass
from concourse import mybir

P = 128
GROUP = 4
TOPK = 350
ALPHA = 0.1
L1_EPS = 1e-12
LN_EPS = 1e-5
TOP_BIT = 29
PER_BIT = 5
STEPS0 = 8
STEPS1 = 14 + PER_BIT * (TOP_BIT + 1)

ALU = mybir.AluOpType
ACT = mybir.ActivationFunctionType
F32 = mybir.dt.float32
BF16 = mybir.dt.bfloat16
I32 = mybir.dt.int32


def gnn_kernel(nc, x, adj, h0, y, w_proj, b_proj, w_gcn, b_gcn, out):
    N, F = x.shape
    C = y.shape[1]
    FULL = N // P
    TAIL = N - FULL * P
    NB = FULL + 1
    NG = -(-NB // GROUP)
    assert F == P and 0 < TAIL <= 32

    def rows_of(b):
        return P if b < FULL else TAIL

    def blocks_of(g):
        return range(g * GROUP, min((g + 1) * GROUP, NB))

    def cols_of(g):
        return slice(g * GROUP * P, min((g + 1) * GROUP * P, N))

    with ExitStack() as ctx:
        def sb(name, shape, dt=F32):
            return ctx.enter_context(nc.sbuf_tensor(name, shape, dt))

        def ps(name, shape, dt=F32):
            return ctx.enter_context(nc.psum_tensor(name, shape, dt))

        def sem(name):
            return ctx.enter_context(nc.semaphore(name))

        ident = sb("ident", [P, P])
        ones = sb("ones", [1, P])
        neg_half = sb("neg_half", [P, 1])
        wp = sb("wp", [F, F])
        wg = sb("wg", [F, F])
        bp_col = sb("bp_col", [F, 1])
        bg_row = sb("bg_row", [1, F])
        bg_all = sb("bg_all", [P, F])
        y_nat = sb("y_nat", [P, NB, C])
        y_t = sb("y_t", [C, N])
        xs = sb("xs", [P, NB, F])
        h0s = sb("h0s", [P, NB, F])
        x1 = sb("x1", [P, NB, F])
        feats = sb("feats", [P, NB, F])
        a_rows = sb("a_rows", [P, N])
        weights = sb("weights", [P, N])
        scratch = sb("scratch", [P, N])
        weights_t = sb("weights_t", [P, NB, P])
        y_block = sb("y_block", [C, P])
        col = sb("col", [P, 16])
        icol = sb("icol", [P, 8], I32)
        stats = sb("stats", [P, 8])
        z = sb("z", [P, F])
        z1 = sb("z1", [P, F])
        xn = sb("xn", [P, F])
        xn_t = sb("xn_t", [F, P])
        h2_t = sb("h2_t", [F, P])
        result = sb("result", [P, F])

        gram = [ps(f"gram{i}", [P, GROUP * P]) for i in range(2)]
        turned = [ps(f"turned{i}", [P, GROUP, P]) for i in range(2)]
        support = ps("support", [P, F])
        small = ps("small", [P, GROUP, P])

        s_const = sem("s_const")
        s_in = [sem(f"s_in{i}") for i in range(9)]
        s_setup_pe = sem("s_setup_pe")
        s_setup_dve = sem("s_setup_dve")
        s_dve = sem("s_dve")
        s_passed = sem("s_passed")
        s_rows = sem("s_rows")
        s_rows_free = sem("s_rows_free")
        s_yblock = sem("s_yblock")
        s_gram = sem("s_gram")
        s_gram_free = sem("s_gram_free")
        s_weighted = sem("s_weighted")
        s_rowsum = sem("s_rowsum")
        s_scaled = sem("s_scaled")
        s_turned = sem("s_turned")
        s_copied = sem("s_copied")
        s_support = sem("s_support")
        s_var = sem("s_var")
        s_rstd = sem("s_rstd")
        s_xn = sem("s_xn")
        s_xnt = sem("s_xnt")
        s_xnt_sb = sem("s_xnt_sb")
        s_proj = sem("s_proj")
        s_h2 = sem("s_h2")
        s_feat = sem("s_feat")
        s_feat_sb = sem("s_feat_sb")
        s_tanh = sem("s_tanh")
        s_result = sem("s_result")
        s_out = sem("s_out")

        def block_view(a):
            return a[0:FULL * P, :].rearrange("(b p) f -> p b f", p=P)

        block = ctx.enter_context(nc.Block())

        def row_range(t, m):
            return bass.ds(t * P, m)

        @block.sync
        def _(sp):
            sp.dma_start(y_nat[:, 0:FULL, :], block_view(y)).then_inc(s_in[0], 16)
            sp.dma_start(y_nat[0:TAIL, FULL, :], y[FULL * P:N, :]).then_inc(s_in[1], 16)
            sp.dma_start(xs[:, 0:FULL, :], block_view(x)).then_inc(s_in[2], 16)
            sp.dma_start(xs[0:TAIL, FULL, :], x[FULL * P:N, :]).then_inc(s_in[3], 16)
            sp.dma_start(h0s[:, 0:FULL, :], block_view(h0)).then_inc(s_in[4], 16)
            sp.dma_start(h0s[0:TAIL, FULL, :], h0[FULL * P:N, :]).then_inc(s_in[5], 16)
            sp.dma_start(wp[:, :], w_proj).then_inc(s_in[6], 16)
            sp.dma_start(wg[:, :], w_gcn).then_inc(s_in[7], 16)
            sp.dma_start(bp_col[:, :], b_proj.rearrange("(p a) -> p a", a=1)).then_inc(s_in[8], 16)
            sp.dma_start(bg_row[:, :], b_gcn.rearrange("(a p) -> a p", a=1)).then_inc(s_in[8], 16)

            def load(t, s, m):
                sp.wait_ge(s_rows_free, s)
                sp.dma_start(a_rows[0:m, :], adj[row_range(t, m), :]).then_inc(s_rows, 16)

            def store(t, m):
                sp.wait_ge(s_result, t + 1)
                sp.dma_start(out[row_range(t, m), :], result[0:m, :]).then_inc(s_out, 16)

            with sp.Fori(0, FULL) as t:
                load(t, t, P)
            load(FULL, FULL, TAIL)
            with sp.Fori(0, FULL) as t:
                load(t, t + NB, P)
                store(t, P)
            load(FULL, FULL + NB, TAIL)
            store(FULL, TAIL)
            sp.wait_ge(s_out, 16 * NB)

        @block.gpsimd
        def _(pool):
            pool.memset(ident[:, :], 0.0).then_inc(s_const, 1)
            pool.memset(ones[:, :], 1.0).then_inc(s_const, 1)
            pool.memset(neg_half[:, :], -0.5).then_inc(s_const, 1)
            pool.wait_ge(s_const, 3)
            pool.affine_select(out=ident[:, :], in_=ident[:, :], compare_op=ALU.not_equal, fill=1.0,
                               base=0, pattern=[[-1, P]], channel_multiplier=1).then_inc(s_const, 1)

            def rstd(s, m):
                pool.wait_ge(s_var, s + 1)
                pool.tensor_tensor(col[0:m, 5:6], col[0:m, 4:5], neg_half[0:m, :], ALU.pow)\
                    .then_inc(s_rstd, 1)

            for first in (0, NB):
                with pool.Fori(first, first + FULL) as s:
                    rstd(s, P)
                rstd(first + FULL, TAIL)

        @block.tensor
        def _(pe):
            pe.wait_ge(s_const, 4)
            pe.wait_ge(s_in[0], 16)
            pe.wait_ge(s_in[1], 16)
            for g in range(NG):
                if g:
                    pe.wait_ge(s_setup_dve, g)
                for b in blocks_of(g):
                    m = rows_of(b)
                    mm = pe.transpose(small[0:C, b % GROUP, 0:m], y_nat[0:m, b, :], ident[0:m, 0:m])
                mm.then_inc(s_setup_pe, 1)
            pe.wait_ge(s_in[8], 32)
            pe.wait_ge(s_setup_dve, NG)
            pe.matmul(small[:, 0, :], ones[:, :], bg_row[:, :], start=True, stop=True)\
                .then_inc(s_setup_pe, 1)
            pe.wait_ge(s_setup_dve, NG + 1)
            for i in (2, 3, 6, 7):
                pe.wait_ge(s_in[i], 16)

            def gram_rows(t, m):
                pe.wait_ge(s_yblock, t + 1)
                for g in range(NG):
                    c = cols_of(g)
                    pe.wait_ge(s_gram_free, t * NG + (g + 1))
                    pe.matmul(gram[g % 2][0:m, 0:c.stop - c.start], y_block[:, 0:m], y_t[:, c],
                              start=True, stop=True).then_inc(s_gram, 1)

            def product(s, m, rhs):
                pe.wait_ge(s_scaled, s + 1)
                for g in range(NG):
                    pe.wait_ge(s_copied, s * NG + (g + 1))
                    for b in blocks_of(g):
                        k = rows_of(b)
                        mm = pe.transpose(turned[g % 2][0:k, b % GROUP, 0:m],
                                          weights[0:m, b * P:b * P + k], ident[0:m, 0:m])
                    mm.then_inc(s_turned, 1)
                pe.wait_ge(s_copied, s * NG + (NG + 2))
                for b in range(NB):
                    k = rows_of(b)
                    mm = pe.matmul(support[0:m, :], weights_t[0:k, b, 0:m], rhs[0:k, b, :],
                                   start=(b == 0), stop=(b == NB - 1))
                mm.then_inc(s_support, 1)

            def layer0(t, m):
                gram_rows(t, m)
                product(t, m, xs)
                pe.wait_ge(s_xn, t + 1)
                pe.transpose(small[:, 0, 0:m], xn[0:m, :], ident[0:m, 0:m]).then_inc(s_xnt, 1)
                pe.wait_ge(s_xnt_sb, t + 1)
                pe.matmul(small[:, 1, 0:m], wp[:, :], xn_t[:, 0:m], start=True, stop=True)\
                    .then_inc(s_proj, 1)
                pe.wait_ge(s_h2, t + 1)
                pe.matmul(small[0:m, 2, :], h2_t[:, 0:m], wg[:, :], start=True, stop=True)\
                    .then_inc(s_feat, 1)

            with pe.Fori(0, FULL) as t:
                layer0(t, P)
            layer0(FULL, TAIL)
            pe.wait_ge(s_feat_sb, NB)
            with pe.Fori(0, FULL) as t:
                product(t + NB, P, feats)
            product(FULL + NB, TAIL, feats)

        @block.scalar
        def _(act):
            def copy_turned(s, m):
                act.wait_ge(s_support, s)
                for g in range(NG):
                    act.wait_ge(s_turned, s * NG + (g + 1))
                    whole = [b for b in blocks_of(g) if b < FULL]
                    if whole:
                        cp = act.activation(weights_t[:, whole[0]:whole[-1] + 1, 0:m],
                                            turned[g % 2][:, 0:len(whole), 0:m], ACT.Copy)
                    if NB - 1 in blocks_of(g):
                        cp = act.activation(weights_t[0:TAIL, FULL, 0:m],
                                            turned[g % 2][0:TAIL, FULL % GROUP, 0:m], ACT.Copy)
                    cp.then_inc(s_copied, 1)

            def layer0(t, m):
                act.wait_ge(s_weighted, t + 1)
                act.activation(a_rows[0:m, :], weights[0:m, :], ACT.Abs, accum_out=col[0:m, 0:1])\
                    .then_inc(s_rowsum, 1)
                copy_turned(t, m)
                act.wait_ge(s_xnt, t + 1)
                act.activation(xn_t[:, 0:m], small[:, 0, 0:m], ACT.Copy).then_inc(s_xnt_sb, 1)
                act.wait_ge(s_proj, t + 1)
                act.activation(h2_t[:, 0:m], small[:, 1, 0:m], ACT.Tanh, bias=bp_col[:, :])\
                    .then_inc(s_h2, 1)

            def layer1(t, m):
                act.wait_ge(s_rows, t * 16 + 16 * (NB + 1))
                act.wait_ge(s_support, t + NB)
                act.activation(weights[0:m, :], a_rows[0:m, :], ACT.Square).then_inc(s_tanh, 1)
                act.wait_ge(s_tanh, t * 2 + 1)
                act.activation(weights[0:m, :], weights[0:m, :], ACT.Tanh).then_inc(s_tanh, 1)
                copy_turned(t + NB, m)

            act.wait_ge(s_in[8], 32)
            with act.Fori(0, FULL) as t:
                layer0(t, P)
            layer0(FULL, TAIL)
            with act.Fori(0, FULL) as t:
                layer1(t, P)
            layer1(FULL, TAIL)

        @block.vector
        def _(dve):
            base = [0, 0]

            def done(ins):
                base[1] += 1
                ins.then_inc(s_dve, 1)
                dve.wait_ge(s_dve, base[0] + base[1])

            for g in range(NG):
                dve.wait_ge(s_setup_pe, g + 1)
                whole = [b for b in blocks_of(g) if b < FULL]
                if whole:
                    cp = dve.tensor_copy(y_t[:, whole[0] * P:(whole[-1] + 1) * P],
                                         small[0:C, 0:len(whole), :].rearrange("c b p -> c (b p)"))
                if NB - 1 in blocks_of(g):
                    cp = dve.tensor_copy(y_t[:, FULL * P:N], small[0:C, FULL % GROUP, 0:TAIL])
                cp.then_inc(s_setup_dve, 1)
            dve.wait_ge(s_setup_pe, NG + 1)
            dve.tensor_copy(bg_all[:, :], small[:, 0, :]).then_inc(s_setup_dve, 1)
            dve.wait_ge(s_setup_dve, NG + 1)
            for i in range(2, 6):
                dve.wait_ge(s_in[i], 16)
            dve.sem_inc(s_gram_free, 2)
            dve.sem_inc(s_copied, 2)

            def layer_norm(s, m, zin, zout):
                done(dve.bn_stats(stats[0:m, 0:6], zin[0:m, :]))
                dve.sem_inc(s_passed, 1)
                done(dve.bn_aggr(col[0:m, 2:4], stats[0:m, 0:6]))
                dve.tensor_scalar(col[0:m, 4:5], col[0:m, 3:4], LN_EPS, None, ALU.add)\
                    .then_inc(s_var, 1)
                dve.wait_ge(s_rstd, s + 1)
                return dve.tensor_scalar(zout[0:m, :], zin[0:m, :], col[0:m, 2:3], col[0:m, 5:6],
                                         ALU.subtract, ALU.mult)

            def at(a, t, m):
                if isinstance(t, int):
                    return a[0:m, t, :]
                return a[0:m, bass.ds(t, 1), :].rearrange("p a f -> p (a f)")

            def layer0(t, m):
                base[:] = [t * STEPS0, 0]
                dve.tensor_copy(y_block[:, 0:m], y_t[:, row_range(t, m)]).then_inc(s_yblock, 1)
                dve.wait_ge(s_rows, t * 16 + 16)
                for g in range(NG):
                    c = cols_of(g)
                    dve.wait_ge(s_gram, t * NG + (g + 1))
                    dve.tensor_tensor(weights[0:m, c], gram[g % 2][0:m, 0:c.stop - c.start],
                                      a_rows[0:m, c], ALU.mult).then_inc(s_gram_free, 1)
                dve.wait_ge(s_gram_free, t * NG + (NG + 2))
                dve.sem_inc(s_weighted, 1)
                dve.wait_ge(s_rowsum, t + 1)
                done(dve.tensor_scalar(col[0:m, 1:2], col[0:m, 0:1], L1_EPS, None, ALU.max))
                done(dve.reciprocal(col[0:m, 1:2], col[0:m, 1:2]))
                done(dve.tensor_scalar(weights[0:m, :], weights[0:m, :], col[0:m, 1:2], None, ALU.mult))
                dve.sem_inc(s_scaled, 1)
                dve.sem_inc(s_rows_free, 1)
                done(dve.scalar_tensor_tensor(z1[0:m, :], at(h0s, t, m), ALPHA, at(xs, t, m),
                                              ALU.mult, ALU.add))
                dve.wait_ge(s_support, t + 1)
                done(dve.scalar_tensor_tensor(z[0:m, :], support[0:m, :], 1.0 - ALPHA, z1[0:m, :],
                                              ALU.mult, ALU.add))
                layer_norm(t, m, z, xn).then_inc(s_xn, 1)
                dve.wait_ge(s_xn, t + 1)
                done(dve.tensor_copy(at(x1, t, m), xn[0:m, :]))
                dve.wait_ge(s_feat, t + 1)
                dve.tensor_copy(at(feats, t, m), small[0:m, 2, :]).then_inc(s_feat_sb, 1)
                assert base[1] == STEPS0

            def layer1(t, m):
                base[:] = [t * STEPS1 + STEPS0 * NB, 0]
                thr, n_ge, n_gt, need = (col[0:m, i:i + 1] for i in range(8, 12))
                cand, bit, mask = (icol[0:m, i:i + 1] for i in range(3))
                dve.wait_ge(s_tanh, t * 2 + 2)
                done(dve.scalar_tensor_tensor(weights[0:m, :], a_rows[0:m, :], 0.0, weights[0:m, :],
                                              ALU.is_gt, ALU.mult))
                done(dve.memset(thr, 0.0))
                done(dve.memset(bit, 1 << TOP_BIT))
                dve.sem_inc(s_passed, 1)
                start = base[0] + base[1]
                with dve.Fori(0, TOP_BIT + 1) as i:
                    base[:] = [start + i * PER_BIT, 0]
                    done(dve.tensor_tensor(cand, thr.bitcast(I32), bit, ALU.bitwise_or))
                    done(dve.tensor_scalar(scratch[0:m, :], weights[0:m, :], cand.bitcast(F32), None,
                                           ALU.is_ge, ALU.add, accum_out=n_ge))
                    done(dve.tensor_scalar(mask, n_ge, float(TOPK), None, ALU.is_ge))
                    dve.sem_inc(s_passed, 1)
                    done(dve.copy_predicated(thr.bitcast(I32), mask, cand))
                    done(dve.tensor_scalar(bit, bit, 1, None, ALU.logical_shift_right))
                    assert base[1] == PER_BIT
                base[:] = [start + PER_BIT * (TOP_BIT + 1), 0]
                done(dve.tensor_scalar(scratch[0:m, :], weights[0:m, :], thr, None,
                                       ALU.is_gt, ALU.add, accum_out=n_gt))
                done(dve.tensor_scalar(need, n_gt, -1.0, float(TOPK), ALU.mult, ALU.add))
                done(dve.tensor_scalar(scratch[0:m, :], weights[0:m, :], thr, None, ALU.is_equal))
                done(dve.tensor_tensor_scan(a_rows[0:m, :], scratch[0:m, :], scratch[0:m, :], 0.0,
                                            ALU.add, ALU.max))
                done(dve.scalar_tensor_tensor(scratch[0:m, :], a_rows[0:m, :], need, scratch[0:m, :],
                                              ALU.is_le, ALU.mult))
                dve.sem_inc(s_rows_free, 1)
                done(dve.scalar_tensor_tensor(scratch[0:m, :], weights[0:m, :], thr, scratch[0:m, :],
                                              ALU.is_gt, ALU.add))
                done(dve.tensor_tensor(weights[0:m, :], weights[0:m, :], scratch[0:m, :], ALU.mult))
                dve.sem_inc(s_scaled, 1)
                dve.wait_ge(s_support, t + (NB + 1))
                done(dve.tensor_tensor(z1[0:m, :], support[0:m, :], bg_all[0:m, :], ALU.add))
                done(dve.scalar_tensor_tensor(z[0:m, :], z1[0:m, :], 0.0, at(x1, t, m),
                                              ALU.max, ALU.add))
                dve.wait_ge(s_out, t * 16)
                layer_norm(t + NB, m, z, result).then_inc(s_result, 1)
                assert start is not None and base[1] == STEPS1 - 3 - PER_BIT * (TOP_BIT + 1)

            with dve.Fori(0, FULL) as t:
                layer0(t, P)
            layer0(FULL, TAIL)
            with dve.Fori(0, FULL) as t:
                layer1(t, P)
            layer1(FULL, TAIL)


_INS = ['x', 'adj', 'L0_gnn_h0', 'L0_gnn_y', 'L1_gnn_W_proj', 'L1_gnn_b_proj', 'L1_gnn_W_gcn', 'L1_gnn_b_gcn']


def kernel(**inputs):
    import numpy as _np
    import concourse.bacc as _bacc
    from concourse import mybir as _mybir
    from concourse.bass_utils import run_bass_kernel_spmd as _run

    nc = _bacc.Bacc("TRN2", target_bir_lowering=False, num_devices=1)
    arrays, args = {}, []
    for name in _INS:
        a = _np.ascontiguousarray(inputs[name])
        arrays[f"in_{name}_dram"] = a
        args.append(nc.dram_tensor(f"in_{name}_dram", a.shape, _mybir.dt.from_np(a.dtype), kind="ExternalInput").ap())
    shape = inputs['x'].shape
    args.append(nc.dram_tensor("out_0_dram", shape, _mybir.dt.from_np(_np.dtype('float32')), kind="ExternalOutput").ap())
    gnn_kernel(nc, *args)
    r = _run(nc, [arrays], core_ids=[0])
    return r.results[0]["out_0_dram"]
```

```python
from contextlib import ExitStack

import concourse.bass as bass
from concourse import mybir

P = 128
GROUP = 4
TOPK = 350
ALPHA = 0.1
L1_EPS = 1e-12
LN_EPS = 1e-5
TOP_BIT = 29
PER_BIT = 5
STEPS0 = 8
STEPS1 = 14 + PER_BIT * (TOP_BIT + 1)

ALU = mybir.AluOpType
ACT = mybir.ActivationFunctionType
F32 = mybir.dt.float32
BF16 = mybir.dt.bfloat16
I32 = mybir.dt.int32
F16 = mybir.dt.float16
U16 = mybir.dt.uint16
AX = mybir.AxisListType

BITS = 16
ONE_BIT = 14
LOW = 2048.0
HUGE = 2.0 ** 63
PART_MAX = 32768.0


def packed_path(nc, x, adj, h0, y, w_proj, b_proj, w_gcn, b_gcn, out, flag):
    N, F = x.shape
    C = y.shape[1]
    FULL = N // P
    TAIL = N - FULL * P
    NB = FULL + 1
    LAST = NB - 1
    WORDS = P // BITS
    HB = (NB + 1) // 2
    HALF = [slice(0, HB * P), slice(HB * P, N)]
    PARTS = 2 * F + 1
    LAG = 4
    assert F == P and 0 < TAIL <= WORDS and C == BITS and FULL % 2 == 1 and FULL > LAG
    assert NB * WORDS <= 512

    def rows_of(b):
        return P if not isinstance(b, int) or b < FULL else TAIL

    def at(a, b, m):
        if isinstance(b, int):
            return a[0:m, b, :]
        return a[0:m, bass.ds(b, 1), :].rearrange("p a f -> p (a f)")

    def at_cols(a, b, m, lo, hi):
        if isinstance(b, int):
            return a[0:m, b, lo:hi]
        return a[0:m, bass.ds(b, 1), lo:hi].rearrange("p a f -> p (a f)")

    def row_range(b, m):
        return bass.ds(b * P, m)

    def steps(eng, step, lag):
        first = max(3, lag + 1 - lag % 2)
        for t in range(first):
            step(t, t % 2, t // 2)
        with eng.Fori((first - 1) // 2, (FULL - 1) // 2) as i:
            step(i * 2 + 1, 1, i)
            step(i * 2 + 2, 0, i + 1)
        for t in range(FULL, NB + lag):
            step(t, t % 2, t // 2)

    def valid(b):
        return not isinstance(b, int) or 0 <= b < NB

    with ExitStack() as ctx:
        def sb(name, shape, dt=F32):
            return ctx.enter_context(nc.sbuf_tensor(name, shape, dt))

        def ps(name, shape, dt=F32):
            return ctx.enter_context(nc.psum_tensor(name, shape, dt))

        def sem(name):
            return ctx.enter_context(nc.semaphore(name))

        ident = sb("ident", [P, P])
        ident_b = sb("ident_b", [P, P], BF16)
        pack = sb("pack", [P, WORDS], BF16)
        ones = sb("ones", [P, P])
        consts = sb("consts", [P, 6])
        neg_half, ln_eps, alpha, low_scale, tanh1, half_tanh1 = (consts[:, i:i + 1] for i in range(6))
        wp = sb("wp", [F, F])
        wg = sb("wg", [F, F])
        bp_col = sb("bp_col", [F, 1])
        bg_row = sb("bg_row", [1, F])
        bg_all = sb("bg_all", [P, F])
        y_nat = sb("y_nat", [P, NB, C])
        xs = sb("xs", [P, NB, F])
        x_parts = sb("x_parts", [P, NB, PARTS + 1], F16)
        f_parts = sb("f_parts", [P, NB, PARTS + 1], F16)
        a_words = sb("a_words", [P, NB, NB * WORDS], U16)
        g_words = sb("g_words", [P, NB, NB * WORDS], U16)
        setup = f_parts[:, :, :].rearrange("p b f -> p (b f)").bitcast(BF16)
        y2_t = setup[0:2 * C, 0:N]
        y2 = setup[:, N:N + NB * 2 * C].rearrange("p (b c) -> p b c", b=NB)
        y_halves = setup[:, N + NB * 2 * C:N + 2 * NB * 2 * C].rearrange("p (b c) -> p b c", b=NB)
        y_packed = sb("y_packed", [2 * C, NB * WORDS], BF16)
        a_rows = [[sb(f"a_rows{p}{h}", [P, HB * P]) for h in range(2)] for p in range(2)]
        a_bits = [sb(f"a_bits{h}", [P, HB * P], BF16) for h in range(2)]
        count_out = sb("count_out", [P, HB * P], BF16)
        turned = sb("turned", [P, 2, NB, P], U16)
        turned_f = turned[:, :, :, :].bitcast(F16)
        x_rest = turned[:, :, :, :].rearrange("p a b f -> p (a b f)").bitcast(F32)
        same_class = sb("same_class", [P, NB * WORDS], U16)
        h0_rows = [sb(f"h0_rows{p}", [P, F]) for p in range(2)]
        h0_part = sb("h0_part", [P, F])
        xh = [sb(f"xh{p}", [P, F]) for p in range(2)]
        low = [sb(f"low{p}", [P, F]) for p in range(2)]
        total = sb("total", [P, F])
        feat = sb("feat", [P, F])
        z = [sb(f"z{p}", [P, F]) for p in range(2)]
        stats = sb("stats", [P, 6])
        rs = sb("rs", [P, 2])
        mean_var = [sb(f"mean_var{p}", [P, 2]) for p in range(2)]
        var_eps = sb("var_eps", [P, 1])
        rstd = [sb(f"rstd{p}", [P, 1]) for p in range(2)]
        xn = [sb(f"xn{p}", [P, F]) for p in range(2)]
        xn_t = sb("xn_t", [F, P])
        h2_t = sb("h2_t", [F, P])
        f_rest = sb("f_rest", [P, F])
        zeros_in = sb("zeros_in", [P, 2 * NB])
        degree = sb("degree", [P, NB])
        good = sb("good", [P, 11])
        chk = sb("chk", [P, NB])

        words = [ps(f"words{p}", [P, 512]) for p in range(2)]
        acc = [ps(f"acc{p}", [P, 512]) for p in range(2)]
        xnt_acc = ps("xnt_acc", [P, 512])
        proj_acc = ps("proj_acc", [P, 512])
        feat_acc = ps("feat_acc", [P, 512])
        y_turned = [a[0:2 * C, 0:2 * P].bitcast(BF16) for a in (proj_acc, feat_acc)]
        gram = [acc[0], acc[1], xnt_acc, proj_acc]

        s_const = sem("s_const")
        s_in = {n: sem(f"s_in_{n}") for n in ("y", "yt", "x", "xt", "wp", "wg", "bp", "bg")}
        s_cleared = sem("s_cleared")
        s_y = sem("s_y")
        s_yt = sem("s_yt")
        s_yt_sb = sem("s_yt_sb")
        s_yp = sem("s_yp")
        s_yp_sb = sem("s_yp_sb")
        s_gram = sem("s_gram")
        s_gram_act = sem("s_gram_act")
        s_gram_dve = sem("s_gram_dve")
        s_bias = sem("s_bias")
        s_bias_sb = sem("s_bias_sb")
        s_xhigh = sem("s_xhigh")
        s_xrest = sem("s_xrest")
        s_xlow = sem("s_xlow")
        s_rows = [[sem(f"s_rows{p}{h}") for h in range(2)] for p in range(2)]
        s_h0 = [sem(f"s_h0{p}") for p in range(2)]
        s_bits = sem("s_bits")
        s_counted = sem("s_counted")
        s_packed = sem("s_packed")
        s_words = sem("s_words")
        s_masked = sem("s_masked")
        s_unpacked = sem("s_unpacked")
        s_acc = sem("s_acc")
        s_low = sem("s_low")
        s_total = sem("s_total")
        s_h0part = sem("s_h0part")
        s_vareps = sem("s_vareps")
        s_floor = sem("s_floor")
        s_inverse = sem("s_inverse")
        s_z = sem("s_z")
        s_bn = sem("s_bn")
        s_biased = sem("s_biased")
        s_tanh1 = sem("s_tanh1")
        s_half = sem("s_half")
        s_all_good = sem("s_all_good")
        s_xh = sem("s_xh")
        s_stats = sem("s_stats")
        s_rstd = sem("s_rstd")
        s_xn = sem("s_xn")
        s_kept = sem("s_kept")
        s_xnt = sem("s_xnt")
        s_xnt_sb = sem("s_xnt_sb")
        s_proj = sem("s_proj")
        s_h2 = sem("s_h2")
        s_feat = sem("s_feat")
        s_high = sem("s_high")
        s_rest = sem("s_rest")
        s_flow = sem("s_flow")
        s_passed = sem("s_passed")
        s_degree = sem("s_degree")
        s_result = sem("s_result")
        s_out = [sem(f"s_out{p}") for p in range(2)]
        s_good = sem("s_good")
        s_sum = sem("s_sum")
        s_flag = sem("s_flag")

        def block_view(a):
            return a[0:FULL * P, :].rearrange("(b p) f -> p b f", p=P)

        def copy_gram(copy, eng, b):
            eng.wait_ge(s_gram, b + 1)
            k = rows_of(b)
            copy(g_words[0:k, :, b * WORDS:(b + 1) * WORDS],
                 gram[b % 4][0:k, 0:NB * WORDS].rearrange("p (i w) -> p i w", w=WORDS))\
                .then_inc(s_gram_dve if b % 2 else s_gram_act, 1)

        block = ctx.enter_context(nc.Block())

        @block.sync
        def _(sp):
            def load_rows(t, par, pair):
                if not valid(t):
                    return
                m = rows_of(t)
                for h in range(2):
                    if not isinstance(t, int) or t >= 2:
                        sp.wait_ge(s_bits, t * 2 - 3 + h)
                        sp.wait_ge(s_counted, t * 2 - 3 + h)
                    sp.dma_start(a_rows[par][h][0:m, 0:HALF[h].stop - HALF[h].start],
                                 adj[row_range(t, m), HALF[h]]).then_inc(s_rows[par][h], 16)

            def load_h0(t, par, pair):
                m = rows_of(t)
                if not isinstance(t, int) or t >= 2:
                    sp.wait_ge(s_xh, t - 1)
                sp.dma_start(h0_rows[par][0:m, :], h0[row_range(t, m), :]).then_inc(s_h0[par], 16)

            sp.dma_start(y_nat[:, 0:FULL, :], block_view(y)).then_inc(s_in["y"], 16)
            load_rows(0, 0, 0)
            sp.wait_ge(s_cleared, 1)
            sp.dma_start(y_nat[0:TAIL, FULL, :], y[FULL * P:N, :]).then_inc(s_in["yt"], 16)
            sp.dma_start(xs[0:TAIL, FULL, :], x[FULL * P:N, :]).then_inc(s_in["xt"], 16)
            sp.dma_start(xs[:, 0:FULL, :], block_view(x)).then_inc(s_in["x"], 16)
            load_rows(1, 1, 0)
            sp.dma_start(wp[:, :], w_proj).then_inc(s_in["wp"], 16)
            sp.dma_start(wg[:, :], w_gcn).then_inc(s_in["wg"], 16)
            sp.dma_start(bp_col[:, :], b_proj.rearrange("(p a) -> p a", a=1)).then_inc(s_in["bp"], 16)
            sp.dma_start(bg_row[:, :], b_gcn.rearrange("(a p) -> a p", a=1)).then_inc(s_in["bg"], 16)

            def step(t, par, pair):
                if isinstance(t, int) and t < 2:
                    load_h0(t, par, pair)
                    return
                load_rows(t, par, pair)
                load_h0(t, par, pair)
            steps(sp, step, 0)

            def store(t, par, pair):
                m = rows_of(t)
                sp.wait_ge(s_result, t + 1)
                sp.dma_start(out[row_range(t, m), :], xn[par][0:m, :]).then_inc(s_out[par], 16)
            steps(sp, store, 0)
            sp.wait_ge(s_out[0], 16 * (NB // 2))
            sp.wait_ge(s_out[1], 16 * (NB // 2))

        @block.gpsimd
        def _(pool):
            pool.memset(ident[:, :], 0.0).then_inc(s_const, 1)
            pool.memset(ident_b[:, :], 0.0).then_inc(s_const, 1)
            pool.memset(pack[:, :], 0.0).then_inc(s_const, 1)
            pool.memset(ones[:, :], 1.0).then_inc(s_const, 1)
            for c, v in ((neg_half, -0.5), (ln_eps, LN_EPS), (alpha, ALPHA), (low_scale, LOW)):
                pool.memset(c, v).then_inc(s_const, 1)
            pool.wait_ge(s_const, 8)
            for tile in (ident, ident_b):
                pool.affine_select(out=tile[:, :], in_=tile[:, :], compare_op=ALU.not_equal, fill=1.0,
                                   base=0, pattern=[[-1, P]], channel_multiplier=1).then_inc(s_const, 1)
            for bit in range(BITS):
                pool.affine_select(out=pack[:, :], in_=pack[:, :], compare_op=ALU.not_equal,
                                   fill=float(1 << bit), base=-bit * WORDS, pattern=[[-1, WORDS]],
                                   channel_multiplier=1).then_inc(s_const, 1)
                pool.wait_ge(s_const, 11 + bit)

            def residual(b, par, pair):
                m = rows_of(b)
                pool.wait_ge(s_h0[par], pair * 16 + 16)
                pool.wait_ge(s_xh, b)
                pool.tensor_tensor(h0_part[0:m, :], h0_rows[par][0:m, :],
                                   alpha[0:m, :].to_broadcast([m, F]), ALU.mult).then_inc(s_h0part, 1)
                pool.wait_ge(s_h0part, b + 1)
                if not isinstance(b, int) or b >= 2:
                    pool.wait_ge(s_z, b - 1)
                pool.tensor_tensor(xh[par][0:m, :], h0_part[0:m, :], at(xs, b, m), ALU.add)\
                    .then_inc(s_xh, 1)

            def inverse_std(n, par, m):
                pool.wait_ge(s_stats, n + 1)
                pool.wait_ge(s_rstd, n)
                pool.tensor_tensor(var_eps[0:m, :], mean_var[par][0:m, 1:2], ln_eps[0:m, :], ALU.add)\
                    .then_inc(s_vareps, 1)
                pool.wait_ge(s_vareps, n + 1)
                pool.tensor_tensor(rstd[par][0:m, :], var_eps[0:m, :], neg_half[0:m, :], ALU.pow)\
                    .then_inc(s_rstd, 1)

            def step(t, par, pair):
                odd = (par + 1) % 2
                if valid(t - 4):
                    m = rows_of(t - 4)
                    pool.wait_ge(s_rest, t - 3)
                    pool.tensor_tensor(at_cols(f_parts, t - 4, m, F, 2 * F), f_rest[0:m, :],
                                       low_scale[0:m, :].to_broadcast([m, F]), ALU.mult)\
                        .then_inc(s_flow, 1)
                if valid(t - 3):
                    m = rows_of(t - 3)
                    pool.wait_ge(s_xn, t - 2)
                    pool.tensor_copy(at(xs, t - 3, m), xn[odd][0:m, :]).then_inc(s_kept, 1)
                if valid(t - 2):
                    inverse_std(t - 2, par, rows_of(t - 2))
                if valid(t):
                    residual(t, par, pair)
            pool.wait_ge(s_in["x"], 16)
            pool.wait_ge(s_in["xt"], 16)
            pool.wait_ge(s_xrest, 1)
            steps(pool, step, LAG)

            def step1(t, par, pair):
                inverse_std(t + NB, par, rows_of(t))
            steps(pool, step1, 0)

        @block.tensor
        def _(pe):
            pe.wait_ge(s_const, 10)
            pe.wait_ge(s_y, 1)
            for b in range(NB):
                if b >= 8 and b % 4 == 0:
                    pe.wait_ge(s_yt_sb, b // 4 - 1)
                m = rows_of(b)
                tr = pe.transpose(y_turned[b // 4 % 2][:, (b % 4) * P:(b % 4) * P + m], y2[0:m, b, :],
                                  ident_b[0:m, 0:m])
                if b % 4 == 3 or b == LAST:
                    tr.then_inc(s_yt, 1)
            pe.wait_ge(s_const, 10 + BITS)
            pe.wait_ge(s_y, 2)
            for b in range(NB):
                mm = pe.matmul(xnt_acc[0:2 * C, b * WORDS:(b + 1) * WORDS], y_halves[:, b, :],
                               pack[:, :], start=True, stop=True)
            mm.then_inc(s_yp, 1)
            pe.wait_ge(s_in["bg"], 16)
            pe.wait_ge(s_yt_sb, -(-NB // 4))
            pe.matmul(feat_acc[:, 0:F], ones[0:1, :], bg_row[:, :], start=True, stop=True)\
                .then_inc(s_bias, 1)
            pe.wait_ge(s_yp_sb, 1)
            for b in range(NB):
                if b >= 4:
                    pe.wait_ge(s_gram_dve if b % 2 else s_gram_act, b // 2 - 1)
                k = rows_of(b)
                pe.matmul(gram[b % 4][0:k, 0:NB * WORDS], y2_t[:, b * P:b * P + k], y_packed[:, :],
                          start=True, stop=True)\
                    .then_inc(s_gram, 1)

            def pack_rows(t, par, m):
                for h in range(2):
                    pe.wait_ge(s_bits, t * 2 + h + 1)
                    if h == 0 and (not isinstance(t, int) or t >= 2):
                        pe.wait_ge(s_words, t - 1)
                    for b in range(h * HB, HB if h == 0 else NB):
                        k = rows_of(b)
                        c = b * P - HALF[h].start
                        mm = pe.matmul(words[par][0:k, b * WORDS:(b + 1) * WORDS],
                                       a_bits[h][0:m, c:c + k], pack[0:m, :], start=True, stop=True)
                    mm.then_inc(s_packed, 1)

            def multiply(n, par, m, parts):
                pe.wait_ge(s_unpacked, n + 1)
                if not isinstance(n, int) or n >= 2:
                    pe.wait_ge(s_total, n - 1)
                for b in range(NB):
                    k = rows_of(b)
                    mm = pe.matmul(acc[par][0:m, 0:PARTS], turned_f[0:k, par, b, 0:m],
                                   parts[0:k, b, 0:PARTS], start=(b == 0), stop=(b == LAST))
                mm.then_inc(s_acc, 1)

            def step(t, par, pair):
                odd = (par + 1) % 2
                if valid(t - 3):
                    m = rows_of(t - 3)
                    pe.wait_ge(s_xn, t - 2)
                    pe.transpose(xnt_acc[:, 0:m], xn[odd][0:m, :], ident[0:m, 0:m]).then_inc(s_xnt, 1)
                if valid(t):
                    pack_rows(t, par, rows_of(t))
                if valid(t - 3):
                    pe.wait_ge(s_xnt_sb, t - 2)
                    pe.matmul(proj_acc[:, 0:m], wp[:, :], xn_t[:, 0:m], start=True, stop=True)\
                        .then_inc(s_proj, 1)
                if valid(t - 4):
                    m = rows_of(t - 4)
                    pe.wait_ge(s_h2, t - 3)
                    if not isinstance(t, int) or t >= 5:
                        pe.wait_ge(s_rest, t - 4)
                    pe.matmul(feat_acc[0:m, 0:F], h2_t[:, 0:m], wg[:, :], start=True, stop=True)\
                        .then_inc(s_feat, 1)
                if valid(t - 1):
                    multiply(t - 1, odd, rows_of(t - 1), x_parts)
            pe.wait_ge(s_gram_act, NB // 2)
            pe.wait_ge(s_gram_dve, NB // 2)
            pe.wait_ge(s_bias_sb, 1)
            pe.wait_ge(s_cleared, 3)
            pe.wait_ge(s_xlow, 1)
            for n in ("wp", "wg"):
                pe.wait_ge(s_in[n], 16)
            steps(pe, step, LAG)
            pe.wait_ge(s_flow, NB)
            steps(pe, lambda t, par, pair: multiply(t + NB, par, rows_of(t), f_parts), 0)
            pe.wait_ge(s_all_good, 1)
            pe.matmul(feat_acc[0:1, 0:1], good[:, 10:11], ones[:, 0:1], start=True, stop=True)\
                .then_inc(s_sum, 1)

        @block.scalar
        def _(act):
            act.wait_ge(s_const, 8)
            act.activation(tanh1, ones[:, 0:1], ACT.Tanh).then_inc(s_tanh1, 1)
            act.wait_ge(s_cleared, 2)
            for b in range(0, NB, 2):
                copy_gram(lambda o, i: act.activation(o, i, ACT.Copy), act, b)
            act.wait_ge(s_in["x"], 16)
            act.wait_ge(s_in["xt"], 16)
            act.activation(x_parts[:, :, 0:F], xs[:, :, :], ACT.Copy).then_inc(s_xhigh, 1)

            def count_zeros(t, par, pair, h, m):
                act.wait_ge(s_rows[par][h], pair * 16 + 16)
                w = HALF[h].stop - HALF[h].start
                col = zeros_in[0:m, bass.ds(t * 2 + h, 1)]
                act.wait_ge(s_counted, t * 2 + h)
                act.activation(count_out[0:m, 0:w], a_rows[par][h][0:m, 0:w], ACT.Relu,
                               bias=ones[0:m, 0:1], scale=-HUGE,
                               accum_out=col).then_inc(s_counted, 1)

            def copy_low(n, par, m):
                if not isinstance(n, int) or n >= 2:
                    act.wait_ge(s_total, n - 1)
                act.wait_ge(s_acc, n + 1)
                act.activation(low[par][0:m, :], acc[par][0:m, F:2 * F], ACT.Copy, scale=1.0 / LOW)\
                    .then_inc(s_low, 1)

            def step(t, par, pair):
                odd = (par + 1) % 2
                if valid(t - 3):
                    m3 = rows_of(t - 3)
                    act.wait_ge(s_xnt, t - 2)
                    act.activation(xn_t[:, 0:m3], xnt_acc[:, 0:m3], ACT.Copy).then_inc(s_xnt_sb, 1)
                if valid(t):
                    count_zeros(t, par, pair, 0, rows_of(t))
                if valid(t - 4):
                    m4 = rows_of(t - 4)
                    act.wait_ge(s_feat, t - 3)
                    act.activation(at_cols(f_parts, t - 4, m4, 0, F), feat_acc[0:m4, 0:F], ACT.Copy)\
                        .then_inc(s_high, 1)
                if valid(t - 2):
                    copy_low(t - 2, par, rows_of(t - 2))
                if valid(t - 3):
                    act.wait_ge(s_proj, t - 2)
                    act.activation(h2_t[:, 0:m3], proj_acc[:, 0:m3], ACT.Tanh, bias=bp_col[:, :])\
                        .then_inc(s_h2, 1)
                if valid(t):
                    count_zeros(t, par, pair, 1, rows_of(t))
                    act.wait_ge(s_packed, t * 2 + 2)
                    act.activation(at(a_words, t, P), words[par][:, 0:NB * WORDS], ACT.Copy)\
                        .then_inc(s_words, 1)
            act.wait_ge(s_in["bp"], 16)
            steps(act, step, LAG)

            def step1(t, par, pair):
                m = rows_of(t)
                act.wait_ge(s_acc, t + (NB + 1))
                act.sem_inc(s_passed, 1)
                act.activation(degree[0:m, bass.ds(t, 1)], acc[par][0:m, 2 * F:2 * F + 1], ACT.Copy,
                               scale=0.5).then_inc(s_degree, 1)
                copy_low(t + NB, par, m)
            steps(act, step1, 0)

        @block.vector
        def _(dve):
            dve.memset(y_nat[:, FULL, :], 0.0)
            dve.memset(xs[:, FULL, :], 0.0).then_inc(s_cleared, 1)
            for p in range(2):
                dve.memset(words[p][:, LAST * WORDS:NB * WORDS], 0.0)
            dve.memset(g_words[:, :, LAST * WORDS:NB * WORDS], 0)
            dve.memset(zeros_in[:, :], N / 2)
            dve.memset(degree[:, :], 0.0)
            dve.memset(x_parts[:, :, 2 * F], 1.0)
            dve.memset(y_halves, 0.0).then_inc(s_cleared, 1)
            dve.wait_ge(s_in["y"], 16)
            dve.wait_ge(s_in["yt"], 16)
            dve.wait_ge(s_cleared, 2)
            dve.tensor_copy(y2[:, :, 0:C], y_nat[:, :, :])
            dve.tensor_copy(y2[:, :, C:2 * C], y_nat[:, :, :]).then_inc(s_y, 1)
            dve.tensor_copy(y_halves[0:P // 2, :, 0:C], y_nat[0:P // 2, :, :])
            dve.tensor_copy(y_halves[P // 2:P, :, C:2 * C], y_nat[P // 2:P, :, :]).then_inc(s_y, 1)
            for g in range(-(-NB // 4)):
                dve.wait_ge(s_yt, g + 1)
                w = min((g + 1) * 4 * P, N) - g * 4 * P
                dve.tensor_copy(y2_t[:, g * 4 * P:g * 4 * P + w],
                                y_turned[g % 2][:, 0:w]).then_inc(s_yt_sb, 1)
            dve.wait_ge(s_yp, 1)
            dve.tensor_copy(y_packed[:, :], xnt_acc[0:2 * C, 0:NB * WORDS]).then_inc(s_yp_sb, 1)
            dve.wait_ge(s_bias, 1)
            dve.tensor_copy(bg_all[:, :], feat_acc[:, 0:F]).then_inc(s_bias_sb, 1)
            for b in range(1, NB, 2):
                copy_gram(dve.tensor_copy, dve, b)
            dve.wait_ge(s_xhigh, 1)
            dve.tensor_tensor(x_rest, xs[:, :, :].rearrange("p b f -> p (b f)"),
                              x_parts[:, :, 0:F], ALU.subtract).then_inc(s_xrest, 1)
            dve.wait_ge(s_xrest, 1)
            dve.tensor_scalar(x_parts[:, :, F:2 * F], x_rest, LOW, None, ALU.mult).then_inc(s_xlow, 1)
            dve.wait_ge(s_xlow, 1)
            dve.wait_ge(s_gram_dve, NB // 2)
            dve.wait_ge(s_gram_act, NB // 2)
            dve.memset(f_parts[:, :, 2 * F], 1.0).then_inc(s_cleared, 1)

            def unpack(n, par, m, source):
                if not isinstance(n, int) or n >= 2:
                    dve.wait_ge(s_acc, n - 1)
                for bit in range(BITS if m == P else 1):
                    shift = ONE_BIT - bit
                    op = ALU.logical_shift_left if shift >= 0 else ALU.logical_shift_right
                    up = dve.tensor_scalar(
                        turned[:, par, :, bit * WORDS:(bit + 1) * WORDS],
                        source.rearrange("p (b w) -> p b w", w=WORDS),
                        abs(shift), 1 << ONE_BIT, op, ALU.bitwise_and)
                up.then_inc(s_unpacked, 1)

            def add_low(n, par, m):
                dve.wait_ge(s_low, n + 1)
                dve.wait_ge(s_z, n)
                dve.tensor_tensor(total[0:m, :], acc[par][0:m, 0:F], low[par][0:m, :], ALU.add)\
                    .then_inc(s_total, 1)
                dve.wait_ge(s_total, n + 1)

            def moments(n, par, m):
                dve.wait_ge(s_z, n + 1)
                dve.wait_ge(s_stats, n)
                dve.bn_stats(stats[0:m, :], z[par][0:m, :]).then_inc(s_bn, 1)
                dve.wait_ge(s_bn, n + 1)
                dve.sem_inc(s_passed, 1)
                dve.bn_aggr(mean_var[par][0:m, :], stats[0:m, :]).then_inc(s_stats, 1)

            def normalize(n, par, m):
                dve.wait_ge(s_rstd, n + 1)
                return dve.tensor_scalar(xn[par][0:m, :], z[par][0:m, :], mean_var[par][0:m, 0:1],
                                         rstd[par][0:m, :], ALU.subtract, ALU.mult)

            def step(t, par, pair):
                odd = (par + 1) % 2
                late = not isinstance(t, int) or t >= 5
                if valid(t - 3):
                    if late:
                        dve.wait_ge(s_xnt, t - 4)
                        dve.wait_ge(s_kept, t - 4)
                    normalize(t - 3, odd, rows_of(t - 3)).then_inc(s_xn, 1)
                if valid(t):
                    m = rows_of(t)
                    for h in range(2):
                        w = HALF[h].stop - HALF[h].start
                        dve.wait_ge(s_rows[par][h], pair * 16 + 16)
                        if not isinstance(t, int) or t >= 1:
                            dve.wait_ge(s_packed, t * 2 - 1 + h)
                        dve.tensor_scalar(a_bits[h][0:m, 0:w], a_rows[par][h][0:m, 0:w], 1.0, None,
                                          ALU.is_equal).then_inc(s_bits, 1)
                if valid(t - 4):
                    m = rows_of(t - 4)
                    dve.wait_ge(s_high, t - 3)
                    if late:
                        dve.wait_ge(s_flow, t - 4)
                    dve.tensor_tensor(f_rest[0:m, :], feat_acc[0:m, 0:F], at_cols(f_parts, t - 4, m, 0, F),
                                      ALU.subtract).then_inc(s_rest, 1)
                if valid(t - 1):
                    dve.wait_ge(s_words, t)
                    dve.wait_ge(s_unpacked, t - 1)
                    dve.tensor_tensor(same_class[:, :], at(a_words, t - 1, P), at(g_words, t - 1, P),
                                      ALU.bitwise_and).then_inc(s_masked, 1)
                    dve.wait_ge(s_masked, t)
                    unpack(t - 1, odd, rows_of(t - 1), same_class[:, :])
                if valid(t - 2):
                    m = rows_of(t - 2)
                    dve.wait_ge(s_low, t - 1)
                    dve.wait_ge(s_z, t - 2)
                    dve.tensor_scalar(rs[0:m, 0:1], acc[par][0:m, 2 * F:2 * F + 1], 2 * L1_EPS,
                                      1 / (1 - ALPHA), ALU.max, ALU.mult).then_inc(s_floor, 1)
                    dve.wait_ge(s_floor, t - 1)
                    dve.reciprocal(rs[0:m, 1:2], rs[0:m, 0:1]).then_inc(s_inverse, 1)
                    add_low(t - 2, par, m)
                    dve.wait_ge(s_inverse, t - 1)
                    dve.wait_ge(s_xh, t - 1)
                    if not isinstance(t, int) or t >= 4:
                        dve.wait_ge(s_xn, t - 3)
                    dve.scalar_tensor_tensor(z[par][0:m, :], total[0:m, :], rs[0:m, 1:2],
                                             xh[par][0:m, :], ALU.mult, ALU.add).then_inc(s_z, 1)
                    moments(t - 2, par, m)
            steps(dve, step, LAG)

            dve.wait_ge(s_tanh1, 1)
            dve.tensor_scalar(half_tanh1, tanh1, 0.5, None, ALU.mult).then_inc(s_half, 1)
            dve.wait_ge(s_half, 1)
            dve.wait_ge(s_kept, NB)
            dve.wait_ge(s_xnt, NB)

            def step1(t, par, pair):
                odd = (par + 1) % 2
                if valid(t):
                    unpack(t + NB, par, rows_of(t), at(a_words, t, P))
                if valid(t - 2):
                    if not isinstance(t, int) or t >= 4:
                        dve.wait_ge(s_out[par], (pair - 1) * 16)
                    normalize(t + (NB - 2), par, rows_of(t - 2)).then_inc(s_result, 1)
                if valid(t - 1):
                    m = rows_of(t - 1)
                    add_low(t + (NB - 1), odd, m)
                    dve.scalar_tensor_tensor(feat[0:m, :], total[0:m, :], half_tanh1[0:m, :],
                                             bg_all[0:m, :], ALU.mult, ALU.add).then_inc(s_biased, 1)
                    dve.wait_ge(s_biased, t)
                    if not isinstance(t, int) or t >= 3:
                        dve.wait_ge(s_result, t - 2)
                    dve.scalar_tensor_tensor(z[odd][0:m, :], feat[0:m, :], 0.0, at(xs, t - 1, m),
                                             ALU.max, ALU.add).then_inc(s_z, 1)
                    moments(t + (NB - 1), odd, m)
            steps(dve, step1, 2)

            k = [0]

            def done(ins):
                k[0] += 1
                ins.then_inc(s_good, 1)
                dve.wait_ge(s_good, k[0])

            dve.wait_ge(s_degree, NB)
            done(dve.memset(chk[:, 0:6], 0.0))
            for i, op in ((0, ALU.max), (3, ALU.min)):
                done(dve.tensor_reduce(chk[:, i:i + 1], x_parts[:, :, 0:F], AX.XY, op))
                done(dve.tensor_reduce(chk[:, i + 1:i + 2], f_parts[:, 0:FULL, 0:F], AX.XY, op))
                done(dve.tensor_reduce(chk[0:TAIL, i + 2:i + 3], f_parts[0:TAIL, FULL, 0:F], AX.X, op))
            done(dve.tensor_scalar(good[:, 0:3], chk[:, 0:3], PART_MAX, None, ALU.is_le))
            done(dve.tensor_scalar(good[:, 3:6], chk[:, 3:6], -PART_MAX, None, ALU.is_ge))
            done(dve.tensor_reduce(chk[:, :], y_nat[:, :, :], AX.X, ALU.add))
            done(dve.tensor_scalar(chk[:, :], chk[:, :], 1.0, None, ALU.is_le))
            done(dve.tensor_reduce(good[:, 6:7], chk[:, :], AX.X, ALU.min))
            done(dve.scalar_tensor_tensor(y_nat[:, :, :].rearrange("p b c -> p (b c)"),
                                          y_nat[:, :, :].rearrange("p b c -> p (b c)"), 1.0,
                                          y_nat[:, :, :].rearrange("p b c -> p (b c)"),
                                          ALU.is_equal, ALU.is_equal, accum_out=chk[:, 0:1]))
            done(dve.tensor_scalar(good[:, 7:8], chk[:, 0:1], float(NB * C), None, ALU.is_equal))
            zeros_in_2 = zeros_in[:, :].rearrange("p (b h) -> p b h", h=2)
            done(dve.tensor_tensor(chk[:, :], zeros_in_2[:, :, 0], zeros_in_2[:, :, 1], ALU.add))
            done(dve.tensor_tensor(chk[:, :], chk[:, :], degree[:, :], ALU.add))
            done(dve.tensor_scalar(chk[:, :], chk[:, :], float(N), None, ALU.is_equal))
            done(dve.tensor_reduce(good[:, 8:9], chk[:, :], AX.X, ALU.min))
            done(dve.tensor_scalar(chk[:, :], degree[:, :], float(TOPK), None, ALU.is_le))
            done(dve.tensor_reduce(good[:, 9:10], chk[:, :], AX.X, ALU.min))
            done(dve.tensor_reduce(good[:, 10:11], good[:, 0:10], AX.X, ALU.min))
            dve.sem_inc(s_all_good, 1)
            dve.wait_ge(s_sum, 1)
            dve.tensor_scalar(flag[:, :], feat_acc[0:1, 0:1], float(P), None, ALU.not_equal)\
                .then_inc(s_flag, 1)


def general_path(nc, x, adj, h0, y, w_proj, b_proj, w_gcn, b_gcn, out, flag):
    N, F = x.shape
    C = y.shape[1]
    FULL = N // P
    TAIL = N - FULL * P
    NB = FULL + 1
    NG = -(-NB // GROUP)
    assert F == P and 0 < TAIL <= 32

    def rows_of(b):
        return P if b < FULL else TAIL

    def blocks_of(g):
        return range(g * GROUP, min((g + 1) * GROUP, NB))

    def cols_of(g):
        return slice(g * GROUP * P, min((g + 1) * GROUP * P, N))

    with ExitStack() as ctx:
        def sb(name, shape, dt=F32):
            return ctx.enter_context(nc.sbuf_tensor(f"general_{name}", shape, dt))

        def ps(name, shape, dt=F32):
            return ctx.enter_context(nc.psum_tensor(f"general_{name}", shape, dt))

        def sem(name):
            return ctx.enter_context(nc.semaphore(f"general_{name}"))

        ident = sb("ident", [P, P])
        ones = sb("ones", [1, P])
        neg_half = sb("neg_half", [P, 1])
        wp = sb("wp", [F, F])
        wg = sb("wg", [F, F])
        bp_col = sb("bp_col", [F, 1])
        bg_row = sb("bg_row", [1, F])
        bg_all = sb("bg_all", [P, F])
        y_nat = sb("y_nat", [P, NB, C])
        y_t = sb("y_t", [C, N])
        xs = sb("xs", [P, NB, F])
        h0s = sb("h0s", [P, NB, F])
        x1 = sb("x1", [P, NB, F])
        feats = sb("feats", [P, NB, F])
        a_rows = sb("a_rows", [P, N])
        weights = sb("weights", [P, N])
        scratch = sb("scratch", [P, N])
        weights_t = sb("weights_t", [P, NB, P])
        y_block = sb("y_block", [C, P])
        col = sb("col", [P, 16])
        icol = sb("icol", [P, 8], I32)
        stats = sb("stats", [P, 8])
        z = sb("z", [P, F])
        z1 = sb("z1", [P, F])
        xn = sb("xn", [P, F])
        xn_t = sb("xn_t", [F, P])
        h2_t = sb("h2_t", [F, P])
        result = sb("result", [P, F])

        gram = [ps(f"gram{i}", [P, GROUP * P]) for i in range(2)]
        turned = [ps(f"turned{i}", [P, GROUP, P]) for i in range(2)]
        support = ps("support", [P, F])
        small = ps("small", [P, GROUP, P])

        s_const = sem("s_const")
        s_in = [sem(f"s_in{i}") for i in range(9)]
        s_setup_pe = sem("s_setup_pe")
        s_setup_dve = sem("s_setup_dve")
        s_dve = sem("s_dve")
        s_passed = sem("s_passed")
        s_rows = sem("s_rows")
        s_rows_free = sem("s_rows_free")
        s_yblock = sem("s_yblock")
        s_gram = sem("s_gram")
        s_gram_free = sem("s_gram_free")
        s_weighted = sem("s_weighted")
        s_rowsum = sem("s_rowsum")
        s_scaled = sem("s_scaled")
        s_turned = sem("s_turned")
        s_copied = sem("s_copied")
        s_support = sem("s_support")
        s_var = sem("s_var")
        s_rstd = sem("s_rstd")
        s_xn = sem("s_xn")
        s_xnt = sem("s_xnt")
        s_xnt_sb = sem("s_xnt_sb")
        s_proj = sem("s_proj")
        s_h2 = sem("s_h2")
        s_feat = sem("s_feat")
        s_feat_sb = sem("s_feat_sb")
        s_tanh = sem("s_tanh")
        s_result = sem("s_result")
        s_out = sem("s_out")

        def block_view(a):
            return a[0:FULL * P, :].rearrange("(b p) f -> p b f", p=P)

        block = ctx.enter_context(nc.Block())

        def row_range(t, m):
            return bass.ds(t * P, m)

        @block.sync
        def _(sp):
            bad = sp.value_load(flag[0:1, 0:1], min_val=0, max_val=1)
            with sp.If(bad != 0):
                sp.dma_start(y_nat[:, 0:FULL, :], block_view(y)).then_inc(s_in[0], 16)
                sp.dma_start(y_nat[0:TAIL, FULL, :], y[FULL * P:N, :]).then_inc(s_in[1], 16)
                sp.dma_start(xs[:, 0:FULL, :], block_view(x)).then_inc(s_in[2], 16)
                sp.dma_start(xs[0:TAIL, FULL, :], x[FULL * P:N, :]).then_inc(s_in[3], 16)
                sp.dma_start(h0s[:, 0:FULL, :], block_view(h0)).then_inc(s_in[4], 16)
                sp.dma_start(h0s[0:TAIL, FULL, :], h0[FULL * P:N, :]).then_inc(s_in[5], 16)
                sp.dma_start(wp[:, :], w_proj).then_inc(s_in[6], 16)
                sp.dma_start(wg[:, :], w_gcn).then_inc(s_in[7], 16)
                sp.dma_start(bp_col[:, :], b_proj.rearrange("(p a) -> p a", a=1)).then_inc(s_in[8], 16)
                sp.dma_start(bg_row[:, :], b_gcn.rearrange("(a p) -> a p", a=1)).then_inc(s_in[8], 16)

                def load(t, s, m):
                    sp.wait_ge(s_rows_free, s)
                    sp.dma_start(a_rows[0:m, :], adj[row_range(t, m), :]).then_inc(s_rows, 16)

                def store(t, m):
                    sp.wait_ge(s_result, t + 1)
                    sp.dma_start(out[row_range(t, m), :], result[0:m, :]).then_inc(s_out, 16)

                with sp.Fori(0, FULL) as t:
                    load(t, t, P)
                load(FULL, FULL, TAIL)
                with sp.Fori(0, FULL) as t:
                    load(t, t + NB, P)
                    store(t, P)
                load(FULL, FULL + NB, TAIL)
                store(FULL, TAIL)
                sp.wait_ge(s_out, 16 * NB)

        @block.gpsimd
        def _(pool):
            bad = pool.value_load(flag[0:1, 0:1], min_val=0, max_val=1)
            with pool.If(bad != 0):
                pool.memset(ident[:, :], 0.0).then_inc(s_const, 1)
                pool.memset(ones[:, :], 1.0).then_inc(s_const, 1)
                pool.memset(neg_half[:, :], -0.5).then_inc(s_const, 1)
                pool.wait_ge(s_const, 3)
                pool.affine_select(out=ident[:, :], in_=ident[:, :], compare_op=ALU.not_equal, fill=1.0,
                                   base=0, pattern=[[-1, P]], channel_multiplier=1).then_inc(s_const, 1)

                def rstd(s, m):
                    pool.wait_ge(s_var, s + 1)
                    pool.tensor_tensor(col[0:m, 5:6], col[0:m, 4:5], neg_half[0:m, :], ALU.pow)\
                        .then_inc(s_rstd, 1)

                for first in (0, NB):
                    with pool.Fori(first, first + FULL) as s:
                        rstd(s, P)
                    rstd(first + FULL, TAIL)

        @block.tensor
        def _(pe):
            bad = pe.value_load(flag[0:1, 0:1], min_val=0, max_val=1)
            with pe.If(bad != 0):
                pe.wait_ge(s_const, 4)
                pe.wait_ge(s_in[0], 16)
                pe.wait_ge(s_in[1], 16)
                for g in range(NG):
                    if g:
                        pe.wait_ge(s_setup_dve, g)
                    for b in blocks_of(g):
                        m = rows_of(b)
                        mm = pe.transpose(small[0:C, b % GROUP, 0:m], y_nat[0:m, b, :], ident[0:m, 0:m])
                    mm.then_inc(s_setup_pe, 1)
                pe.wait_ge(s_in[8], 32)
                pe.wait_ge(s_setup_dve, NG)
                pe.matmul(small[:, 0, :], ones[:, :], bg_row[:, :], start=True, stop=True)\
                    .then_inc(s_setup_pe, 1)
                pe.wait_ge(s_setup_dve, NG + 1)
                for i in (2, 3, 6, 7):
                    pe.wait_ge(s_in[i], 16)

                def gram_rows(t, m):
                    pe.wait_ge(s_yblock, t + 1)
                    for g in range(NG):
                        c = cols_of(g)
                        pe.wait_ge(s_gram_free, t * NG + (g + 1))
                        pe.matmul(gram[g % 2][0:m, 0:c.stop - c.start], y_block[:, 0:m], y_t[:, c],
                                  start=True, stop=True).then_inc(s_gram, 1)

                def product(s, m, rhs):
                    pe.wait_ge(s_scaled, s + 1)
                    for g in range(NG):
                        pe.wait_ge(s_copied, s * NG + (g + 1))
                        for b in blocks_of(g):
                            k = rows_of(b)
                            mm = pe.transpose(turned[g % 2][0:k, b % GROUP, 0:m],
                                              weights[0:m, b * P:b * P + k], ident[0:m, 0:m])
                        mm.then_inc(s_turned, 1)
                    pe.wait_ge(s_copied, s * NG + (NG + 2))
                    for b in range(NB):
                        k = rows_of(b)
                        mm = pe.matmul(support[0:m, :], weights_t[0:k, b, 0:m], rhs[0:k, b, :],
                                       start=(b == 0), stop=(b == NB - 1))
                    mm.then_inc(s_support, 1)

                def layer0(t, m):
                    gram_rows(t, m)
                    product(t, m, xs)
                    pe.wait_ge(s_xn, t + 1)
                    pe.transpose(small[:, 0, 0:m], xn[0:m, :], ident[0:m, 0:m]).then_inc(s_xnt, 1)
                    pe.wait_ge(s_xnt_sb, t + 1)
                    pe.matmul(small[:, 1, 0:m], wp[:, :], xn_t[:, 0:m], start=True, stop=True)\
                        .then_inc(s_proj, 1)
                    pe.wait_ge(s_h2, t + 1)
                    pe.matmul(small[0:m, 2, :], h2_t[:, 0:m], wg[:, :], start=True, stop=True)\
                        .then_inc(s_feat, 1)

                with pe.Fori(0, FULL) as t:
                    layer0(t, P)
                layer0(FULL, TAIL)
                pe.wait_ge(s_feat_sb, NB)
                with pe.Fori(0, FULL) as t:
                    product(t + NB, P, feats)
                product(FULL + NB, TAIL, feats)

        @block.scalar
        def _(act):
            bad = act.value_load(flag[0:1, 0:1], min_val=0, max_val=1)
            with act.If(bad != 0):
                def copy_turned(s, m):
                    act.wait_ge(s_support, s)
                    for g in range(NG):
                        act.wait_ge(s_turned, s * NG + (g + 1))
                        whole = [b for b in blocks_of(g) if b < FULL]
                        if whole:
                            cp = act.activation(weights_t[:, whole[0]:whole[-1] + 1, 0:m],
                                                turned[g % 2][:, 0:len(whole), 0:m], ACT.Copy)
                        if NB - 1 in blocks_of(g):
                            cp = act.activation(weights_t[0:TAIL, FULL, 0:m],
                                                turned[g % 2][0:TAIL, FULL % GROUP, 0:m], ACT.Copy)
                        cp.then_inc(s_copied, 1)

                def layer0(t, m):
                    act.wait_ge(s_weighted, t + 1)
                    act.activation(a_rows[0:m, :], weights[0:m, :], ACT.Abs, accum_out=col[0:m, 0:1])\
                        .then_inc(s_rowsum, 1)
                    copy_turned(t, m)
                    act.wait_ge(s_xnt, t + 1)
                    act.activation(xn_t[:, 0:m], small[:, 0, 0:m], ACT.Copy).then_inc(s_xnt_sb, 1)
                    act.wait_ge(s_proj, t + 1)
                    act.activation(h2_t[:, 0:m], small[:, 1, 0:m], ACT.Tanh, bias=bp_col[:, :])\
                        .then_inc(s_h2, 1)

                def layer1(t, m):
                    act.wait_ge(s_rows, t * 16 + 16 * (NB + 1))
                    act.wait_ge(s_support, t + NB)
                    act.activation(weights[0:m, :], a_rows[0:m, :], ACT.Square).then_inc(s_tanh, 1)
                    act.wait_ge(s_tanh, t * 2 + 1)
                    act.activation(weights[0:m, :], weights[0:m, :], ACT.Tanh).then_inc(s_tanh, 1)
                    copy_turned(t + NB, m)

                act.wait_ge(s_in[8], 32)
                with act.Fori(0, FULL) as t:
                    layer0(t, P)
                layer0(FULL, TAIL)
                with act.Fori(0, FULL) as t:
                    layer1(t, P)
                layer1(FULL, TAIL)

        @block.vector
        def _(dve):
            bad = dve.value_load(flag[0:1, 0:1], min_val=0, max_val=1)
            with dve.If(bad != 0):
                base = [0, 0]

                def done(ins):
                    base[1] += 1
                    ins.then_inc(s_dve, 1)
                    dve.wait_ge(s_dve, base[0] + base[1])

                for g in range(NG):
                    dve.wait_ge(s_setup_pe, g + 1)
                    whole = [b for b in blocks_of(g) if b < FULL]
                    if whole:
                        cp = dve.tensor_copy(y_t[:, whole[0] * P:(whole[-1] + 1) * P],
                                             small[0:C, 0:len(whole), :].rearrange("c b p -> c (b p)"))
                    if NB - 1 in blocks_of(g):
                        cp = dve.tensor_copy(y_t[:, FULL * P:N], small[0:C, FULL % GROUP, 0:TAIL])
                    cp.then_inc(s_setup_dve, 1)
                dve.wait_ge(s_setup_pe, NG + 1)
                dve.tensor_copy(bg_all[:, :], small[:, 0, :]).then_inc(s_setup_dve, 1)
                dve.wait_ge(s_setup_dve, NG + 1)
                for i in range(2, 6):
                    dve.wait_ge(s_in[i], 16)
                dve.sem_inc(s_gram_free, 2)
                dve.sem_inc(s_copied, 2)

                def layer_norm(s, m, zin, zout):
                    done(dve.bn_stats(stats[0:m, 0:6], zin[0:m, :]))
                    dve.sem_inc(s_passed, 1)
                    done(dve.bn_aggr(col[0:m, 2:4], stats[0:m, 0:6]))
                    dve.tensor_scalar(col[0:m, 4:5], col[0:m, 3:4], LN_EPS, None, ALU.add)\
                        .then_inc(s_var, 1)
                    dve.wait_ge(s_rstd, s + 1)
                    return dve.tensor_scalar(zout[0:m, :], zin[0:m, :], col[0:m, 2:3], col[0:m, 5:6],
                                             ALU.subtract, ALU.mult)

                def at(a, t, m):
                    if isinstance(t, int):
                        return a[0:m, t, :]
                    return a[0:m, bass.ds(t, 1), :].rearrange("p a f -> p (a f)")

                def layer0(t, m):
                    base[:] = [t * STEPS0, 0]
                    dve.tensor_copy(y_block[:, 0:m], y_t[:, row_range(t, m)]).then_inc(s_yblock, 1)
                    dve.wait_ge(s_rows, t * 16 + 16)
                    for g in range(NG):
                        c = cols_of(g)
                        dve.wait_ge(s_gram, t * NG + (g + 1))
                        dve.tensor_tensor(weights[0:m, c], gram[g % 2][0:m, 0:c.stop - c.start],
                                          a_rows[0:m, c], ALU.mult).then_inc(s_gram_free, 1)
                    dve.wait_ge(s_gram_free, t * NG + (NG + 2))
                    dve.sem_inc(s_weighted, 1)
                    dve.wait_ge(s_rowsum, t + 1)
                    done(dve.tensor_scalar(col[0:m, 1:2], col[0:m, 0:1], L1_EPS, None, ALU.max))
                    done(dve.reciprocal(col[0:m, 1:2], col[0:m, 1:2]))
                    done(dve.tensor_scalar(weights[0:m, :], weights[0:m, :], col[0:m, 1:2], None, ALU.mult))
                    dve.sem_inc(s_scaled, 1)
                    dve.sem_inc(s_rows_free, 1)
                    done(dve.scalar_tensor_tensor(z1[0:m, :], at(h0s, t, m), ALPHA, at(xs, t, m),
                                                  ALU.mult, ALU.add))
                    dve.wait_ge(s_support, t + 1)
                    done(dve.scalar_tensor_tensor(z[0:m, :], support[0:m, :], 1.0 - ALPHA, z1[0:m, :],
                                                  ALU.mult, ALU.add))
                    layer_norm(t, m, z, xn).then_inc(s_xn, 1)
                    dve.wait_ge(s_xn, t + 1)
                    done(dve.tensor_copy(at(x1, t, m), xn[0:m, :]))
                    dve.wait_ge(s_feat, t + 1)
                    dve.tensor_copy(at(feats, t, m), small[0:m, 2, :]).then_inc(s_feat_sb, 1)
                    assert base[1] == STEPS0

                def layer1(t, m):
                    base[:] = [t * STEPS1 + STEPS0 * NB, 0]
                    thr, n_ge, n_gt, need = (col[0:m, i:i + 1] for i in range(8, 12))
                    cand, bit, mask = (icol[0:m, i:i + 1] for i in range(3))
                    dve.wait_ge(s_tanh, t * 2 + 2)
                    done(dve.scalar_tensor_tensor(weights[0:m, :], a_rows[0:m, :], 0.0, weights[0:m, :],
                                                  ALU.is_gt, ALU.mult))
                    done(dve.memset(thr, 0.0))
                    done(dve.memset(bit, 1 << TOP_BIT))
                    dve.sem_inc(s_passed, 1)
                    start = base[0] + base[1]
                    with dve.Fori(0, TOP_BIT + 1) as i:
                        base[:] = [start + i * PER_BIT, 0]
                        done(dve.tensor_tensor(cand, thr.bitcast(I32), bit, ALU.bitwise_or))
                        done(dve.tensor_scalar(scratch[0:m, :], weights[0:m, :], cand.bitcast(F32), None,
                                               ALU.is_ge, ALU.add, accum_out=n_ge))
                        done(dve.tensor_scalar(mask, n_ge, float(TOPK), None, ALU.is_ge))
                        dve.sem_inc(s_passed, 1)
                        done(dve.copy_predicated(thr.bitcast(I32), mask, cand))
                        done(dve.tensor_scalar(bit, bit, 1, None, ALU.logical_shift_right))
                        assert base[1] == PER_BIT
                    base[:] = [start + PER_BIT * (TOP_BIT + 1), 0]
                    done(dve.tensor_scalar(scratch[0:m, :], weights[0:m, :], thr, None,
                                           ALU.is_gt, ALU.add, accum_out=n_gt))
                    done(dve.tensor_scalar(need, n_gt, -1.0, float(TOPK), ALU.mult, ALU.add))
                    done(dve.tensor_scalar(scratch[0:m, :], weights[0:m, :], thr, None, ALU.is_equal))
                    done(dve.tensor_tensor_scan(a_rows[0:m, :], scratch[0:m, :], scratch[0:m, :], 0.0,
                                                ALU.add, ALU.max))
                    done(dve.scalar_tensor_tensor(scratch[0:m, :], a_rows[0:m, :], need, scratch[0:m, :],
                                                  ALU.is_le, ALU.mult))
                    dve.sem_inc(s_rows_free, 1)
                    done(dve.scalar_tensor_tensor(scratch[0:m, :], weights[0:m, :], thr, scratch[0:m, :],
                                                  ALU.is_gt, ALU.add))
                    done(dve.tensor_tensor(weights[0:m, :], weights[0:m, :], scratch[0:m, :], ALU.mult))
                    dve.sem_inc(s_scaled, 1)
                    dve.wait_ge(s_support, t + (NB + 1))
                    done(dve.tensor_tensor(z1[0:m, :], support[0:m, :], bg_all[0:m, :], ALU.add))
                    done(dve.scalar_tensor_tensor(z[0:m, :], z1[0:m, :], 0.0, at(x1, t, m),
                                                  ALU.max, ALU.add))
                    dve.wait_ge(s_out, t * 16)
                    layer_norm(t + NB, m, z, result).then_inc(s_result, 1)
                    assert start is not None and base[1] == STEPS1 - 3 - PER_BIT * (TOP_BIT + 1)

                with dve.Fori(0, FULL) as t:
                    layer0(t, P)
                layer0(FULL, TAIL)
                with dve.Fori(0, FULL) as t:
                    layer1(t, P)
                layer1(FULL, TAIL)



def gnn_kernel(nc, x, adj, h0, y, w_proj, b_proj, w_gcn, b_gcn, out):
    with nc.sbuf_tensor("flag", [1, 1], I32) as flag:
        packed_path(nc, x, adj, h0, y, w_proj, b_proj, w_gcn, b_gcn, out, flag)
        general_path(nc, x, adj, h0, y, w_proj, b_proj, w_gcn, b_gcn, out, flag)


_INS = ['x', 'adj', 'L0_gnn_h0', 'L0_gnn_y', 'L1_gnn_W_proj', 'L1_gnn_b_proj', 'L1_gnn_W_gcn', 'L1_gnn_b_gcn']


def kernel(**inputs):
    import numpy as _np
    import concourse.bacc as _bacc
    from concourse import mybir as _mybir
    from concourse.bass_utils import run_bass_kernel_spmd as _run

    nc = _bacc.Bacc("TRN2", target_bir_lowering=False, num_devices=1)
    arrays, args = {}, []
    for name in _INS:
        a = _np.ascontiguousarray(inputs[name])
        arrays[f"in_{name}_dram"] = a
        args.append(nc.dram_tensor(f"in_{name}_dram", a.shape, _mybir.dt.from_np(a.dtype), kind="ExternalInput").ap())
    shape = inputs['x'].shape
    args.append(nc.dram_tensor("out_0_dram", shape, _mybir.dt.from_np(_np.dtype('float32')), kind="ExternalOutput").ap())
    gnn_kernel(nc, *args)
    r = _run(nc, [arrays], core_ids=[0])
    return r.results[0]["out_0_dram"]
```

```python
from contextlib import ExitStack

import concourse.bass as bass
from concourse import mybir

P = 128
GROUP = 4
TOPK = 350
ALPHA = 0.1
L1_EPS = 1e-12
LN_EPS = 1e-5
TOP_BIT = 29
PER_BIT = 5
STEPS0 = 8
STEPS1 = 14 + PER_BIT * (TOP_BIT + 1)

ALU = mybir.AluOpType
ACT = mybir.ActivationFunctionType
F32 = mybir.dt.float32
BF16 = mybir.dt.bfloat16
I32 = mybir.dt.int32
F16 = mybir.dt.float16
U16 = mybir.dt.uint16
AX = mybir.AxisListType

BITS = 16
ONE_BIT = 14
LOW = 2048.0
HUGE = 2.0 ** 63
PART_MAX = 32768.0


def packed_path(nc, x, adj, h0, y, w_proj, b_proj, w_gcn, b_gcn, out, flag):
    N, F = x.shape
    C = y.shape[1]
    FULL = N // P
    TAIL = N - FULL * P
    NB = FULL + 1
    LAST = NB - 1
    WORDS = P // BITS
    HB = (NB + 1) // 2
    HALF = [slice(0, HB * P), slice(HB * P, N)]
    PARTS = 2 * F + 2
    CHECKS = 11
    EARLY = NB - 4
    CUT = (EARLY // 12, EARLY // 5, EARLY * 4 // 7)
    LAG = 7
    assert F == P and 0 < TAIL <= WORDS and C == BITS and FULL % 2 == 1 and FULL > LAG
    assert NB * WORDS <= 512 and NB % 4 == 0

    def block(t):
        return LAST if isinstance(t, int) and t == 0 else t - 1

    def rows_in(b):
        return TAIL if isinstance(b, int) and b == LAST else P

    def rows_of(t):
        return rows_in(block(t))

    def at(a, b, m):
        if isinstance(b, int):
            return a[0:m, b, :]
        return a[0:m, bass.ds(b, 1), :].rearrange("p a f -> p (a f)")

    def at_cols(a, b, m, lo, hi):
        if isinstance(b, int):
            return a[0:m, b, lo:hi]
        return a[0:m, bass.ds(b, 1), lo:hi].rearrange("p a f -> p (a f)")

    def row_range(b, m):
        return bass.ds(b * P, m)

    def steps(eng, step, lag, after={}):
        first = max(3, lag + 1 + lag % 2)
        for t in range(first):
            step(t, t % 2, t // 2)
            if t in after:
                after[t]()
        with eng.Fori((first - 1) // 2, (FULL - 1) // 2) as i:
            step(i * 2 + 1, 1, i)
            step(i * 2 + 2, 0, i + 1)
        for t in range(FULL, NB + lag):
            step(t, t % 2, t // 2)

    def valid(b):
        return not isinstance(b, int) or 0 <= b < NB

    with ExitStack() as ctx:
        def sb(name, shape, dt=F32):
            return ctx.enter_context(nc.sbuf_tensor(name, shape, dt))

        def ps(name, shape, dt=F32):
            return ctx.enter_context(nc.psum_tensor(name, shape, dt))

        def sem(name):
            return ctx.enter_context(nc.semaphore(name))

        ident = sb("ident", [P, P])
        ident_b = sb("ident_b", [P, P], BF16)
        pack = sb("pack", [P, WORDS], BF16)
        ones = sb("ones", [P, P])
        consts = sb("consts", [P, 7])
        neg_half, ln_eps, alpha, low_scale, tanh1, half_tanh1, low_tanh1 = (
            consts[:, i:i + 1] for i in range(7))
        wp = sb("wp", [F, F])
        wg = sb("wg", [F, F])
        bp_col = sb("bp_col", [F, 1])
        bg_row = sb("bg_row", [1, F])
        bg_all = sb("bg_all", [P, F])
        y_nat = sb("y_nat", [P, NB, C])
        xs = sb("xs", [P, NB, F])
        x_parts = sb("x_parts", [P, NB, PARTS], F16)
        f_parts = sb("f_parts", [P, NB, PARTS], F16)
        a_words = sb("a_words", [P, NB, NB * WORDS], U16)
        g_words = sb("g_words", [P, NB, NB * WORDS], U16)
        setup = f_parts[:, :, :].rearrange("p b f -> p (b f)").bitcast(BF16)
        y2_t = setup[0:2 * C, 0:N]
        y2 = setup[:, N:N + NB * 2 * C].rearrange("p (b c) -> p b c", b=NB)
        y_halves = setup[:, N + NB * 2 * C:N + 2 * NB * 2 * C].rearrange("p (b c) -> p b c", b=NB)
        y_packed = sb("y_packed", [2 * C, NB * WORDS], BF16)
        a_rows = [[sb(f"a_rows{p}{h}", [P, HB * P]) for h in range(2)] for p in range(2)]
        turned_more = a_rows[0][0][:, :].bitcast(U16).rearrange("p (b i) -> p b i", b=NB)
        a_bits = [sb(f"a_bits{h}", [P, HB * P], BF16) for h in range(2)]
        count_out = sb("count_out", [P, HB * P], BF16)
        turned = sb("turned", [P, 2, NB, P], U16)
        x_rest = turned[:, 1, :, :].rearrange("p b f -> p (b f)").bitcast(F32)
        X_HALF = (slice(0, NB // 2), slice(NB // 2, NB))
        same_class = sb("same_class", [P, NB * WORDS], U16)
        h0_rows = [sb(f"h0_rows{p}", [P, F]) for p in range(2)]
        h0_part = sb("h0_part", [P, F])
        xh = [sb(f"xh{p}", [P, F]) for p in range(2)]
        z_high = sb("z_high", [P, F])
        low_feat = sb("low_feat", [P, F])
        feat = sb("feat", [P, F])
        z = [sb(f"z{p}", [P, F]) for p in range(2)]
        stats = sb("stats", [P, 6])
        rs = sb("rs", [P, 4])
        mean_var = [sb(f"mean_var{p}", [P, 2]) for p in range(2)]
        var_eps = sb("var_eps", [P, 1])
        rstd = [sb(f"rstd{p}", [P, 1]) for p in range(2)]
        xn = [sb(f"xn{p}", [P, F]) for p in range(2)]
        xn_t = sb("xn_t", [F, P])
        h2_t = sb("h2_t", [F, P])
        f_rest = sb("f_rest", [P, F])
        zeros_in = sb("zeros_in", [P, 2 * NB])
        degree = sb("degree", [P, NB])
        x_sums = sb("x_sums", [P, NB])
        f_sums = sb("f_sums", [P, NB])
        square_out = sb("square_out", [P, F], BF16)
        need = sb("need", [P, NB])
        chk = sb("chk", [P, NB])
        holds = sb("holds", [P, 6, NB])
        good = sb("good", [P, 1])

        words = [ps(f"words{p}", [P, 512]) for p in range(2)]
        acc = [ps(f"acc{p}", [P, 512]) for p in range(2)]
        xnt_acc = ps("xnt_acc", [P, 512])
        proj_acc = ps("proj_acc", [P, 512])
        feat_acc = ps("feat_acc", [P, 512])
        y_turned = [a[0:2 * C, 0:2 * P].bitcast(BF16) for a in (proj_acc, feat_acc)]
        gram = [acc[0], acc[1], xnt_acc, proj_acc]

        s_const = sem("s_const")
        s_in = {n: sem(f"s_in_{n}") for n in ("y", "yt", "x", "xt", "wp", "wg", "bp", "bg")}
        s_cleared = sem("s_cleared")
        s_y = sem("s_y")
        s_yt = sem("s_yt")
        s_yt_sb = sem("s_yt_sb")
        s_yp = sem("s_yp")
        s_yp_sb = sem("s_yp_sb")
        s_gram = sem("s_gram")
        s_gram_act = sem("s_gram_act")
        s_gram_dve = sem("s_gram_dve")
        s_bias = sem("s_bias")
        s_bias_sb = sem("s_bias_sb")
        s_xhigh = sem("s_xhigh")
        s_xrest = sem("s_xrest")
        s_xlow = sem("s_xlow")
        s_rows = [[sem(f"s_rows{p}{h}") for h in range(2)] for p in range(2)]
        s_h0 = [sem(f"s_h0{p}") for p in range(2)]
        s_bits = sem("s_bits")
        s_counted = sem("s_counted")
        s_packed = sem("s_packed")
        s_words = sem("s_words")
        s_masked = sem("s_masked")
        s_unpacked = sem("s_unpacked")
        s_acc = sem("s_acc")
        s_zhigh = sem("s_zhigh")
        s_lowfeat = sem("s_lowfeat")
        s_measured = sem("s_measured")
        s_h0part = sem("s_h0part")
        s_vareps = sem("s_vareps")
        s_floor = sem("s_floor")
        s_inverse = sem("s_inverse")
        s_z = sem("s_z")
        s_bn = sem("s_bn")
        s_biased = sem("s_biased")
        s_tanh1 = sem("s_tanh1")
        s_half = sem("s_half")
        s_xh = sem("s_xh")
        s_stats = sem("s_stats")
        s_rstd = sem("s_rstd")
        s_xn = sem("s_xn")
        s_kept = sem("s_kept")
        s_xnt = sem("s_xnt")
        s_xnt_sb = sem("s_xnt_sb")
        s_proj = sem("s_proj")
        s_h2 = sem("s_h2")
        s_feat = sem("s_feat")
        s_high = sem("s_high")
        s_rest = sem("s_rest")
        s_flow = sem("s_flow")
        s_passed = sem("s_passed")
        s_degree = sem("s_degree")
        s_result = sem("s_result")
        s_out = [sem(f"s_out{p}") for p in range(2)]
        s_good = sem("s_good")
        s_sum = sem("s_sum")
        s_flag = sem("s_flag")

        def turned_at(n, par):
            return turned_more if isinstance(n, int) and n == NB + 2 else turned[:, par, :, :]

        def block_view(a):
            return a[0:FULL * P, :].rearrange("(b p) f -> p b f", p=P)

        GRAM = (range(NB // 2 + 4), range(NB // 2 + 4, NB))
        GRAM_DVE = [b for b in range(NB) if b < NB // 4 or b % 2 or b in GRAM[1][:4]]
        GRAM_ACT = [b for b in range(NB) if b not in GRAM_DVE]

        def gram_copied(b):
            owner, s_done = (GRAM_DVE, s_gram_dve) if b in GRAM_DVE else (GRAM_ACT, s_gram_act)
            return s_done, owner.index(b) + 1

        def copy_gram(copy, eng, b):
            eng.wait_ge(s_gram, b + 1)
            k = rows_in(b)
            copy(g_words[0:k, :, b * WORDS:(b + 1) * WORDS],
                 gram[b % 4][0:k, 0:NB * WORDS].rearrange("p (i w) -> p i w", w=WORDS))\
                .then_inc(gram_copied(b)[0], 1)

        engines = ctx.enter_context(nc.Block())

        @engines.sync
        def _(sp):
            def load_rows(t, par, pair):
                if not valid(t):
                    return
                m = rows_of(t)
                for h in range(2):
                    if not isinstance(t, int) or t >= 2:
                        sp.wait_ge(s_bits, t * 2 - 3 + h)
                        sp.wait_ge(s_counted, t * 2 - 3 + h)
                    sp.dma_start(a_rows[par][h][0:m, 0:HALF[h].stop - HALF[h].start],
                                 adj[row_range(block(t), m), HALF[h]]).then_inc(s_rows[par][h], 16)

            def load_h0(n, par):
                m = rows_of(n)
                if not isinstance(n, int) or n >= 2:
                    sp.wait_ge(s_xh, n - 1)
                sp.dma_start(h0_rows[par][0:m, :], h0[row_range(block(n), m), :]).then_inc(s_h0[par], 16)

            sp.dma_start(y_nat[:, 0:FULL, :], block_view(y)).then_inc(s_in["y"], 16)
            sp.wait_ge(s_cleared, 1)
            sp.dma_start(y_nat[0:TAIL, FULL, :], y[FULL * P:N, :]).then_inc(s_in["yt"], 16)
            load_rows(0, 0, 0)
            sp.dma_start(xs[0:TAIL, FULL, :], x[FULL * P:N, :]).then_inc(s_in["xt"], 16)
            sp.dma_start(xs[:, 0:FULL, :], block_view(x)).then_inc(s_in["x"], 16)
            load_rows(1, 1, 0)
            sp.dma_start(wp[:, :], w_proj).then_inc(s_in["wp"], 16)
            sp.dma_start(wg[:, :], w_gcn).then_inc(s_in["wg"], 16)
            sp.dma_start(bp_col[:, :], b_proj.rearrange("(p a) -> p a", a=1)).then_inc(s_in["bp"], 16)
            sp.dma_start(bg_row[:, :], b_gcn.rearrange("(a p) -> a p", a=1)).then_inc(s_in["bg"], 16)

            def step(t, par, pair):
                if not isinstance(t, int) or t >= 2:
                    load_rows(t, par, pair)
                if valid(t - 2):
                    load_h0(t - 2, par)
            steps(sp, step, 4)

            def store(t, par, pair):
                m = rows_of(t)
                sp.wait_ge(s_result, t + 1)
                sp.dma_start(out[row_range(block(t), m), :], xn[par][0:m, :]).then_inc(s_out[par], 16)
            steps(sp, store, 0)
            sp.wait_ge(s_out[0], 16 * (NB // 2))
            sp.wait_ge(s_out[1], 16 * (NB // 2))

        @engines.gpsimd
        def _(pool):
            pool.memset(ident[:, :], 0.0).then_inc(s_const, 1)
            pool.memset(ident_b[:, :], 0.0).then_inc(s_const, 1)
            pool.memset(pack[:, :], 0.0).then_inc(s_const, 1)
            pool.memset(ones[:, :], 1.0).then_inc(s_const, 1)
            for c, v in ((neg_half, -0.5), (ln_eps, LN_EPS), (alpha, ALPHA), (low_scale, LOW)):
                pool.memset(c, v).then_inc(s_const, 1)
            pool.wait_ge(s_const, 8)
            for tile in (ident, ident_b):
                pool.affine_select(out=tile[:, :], in_=tile[:, :], compare_op=ALU.not_equal, fill=1.0,
                                   base=0, pattern=[[-1, P]], channel_multiplier=1).then_inc(s_const, 1)
            for bit in range(BITS):
                pool.affine_select(out=pack[:, :], in_=pack[:, :], compare_op=ALU.not_equal,
                                   fill=float(1 << bit), base=-bit * WORDS, pattern=[[-1, WORDS]],
                                   channel_multiplier=1).then_inc(s_const, 1)
                pool.wait_ge(s_const, 11 + bit)

            def residual(n, par, pair):
                m = rows_of(n)
                pool.wait_ge(s_h0[par], pair * 16 + 16)
                pool.wait_ge(s_xh, n)
                pool.tensor_tensor(h0_part[0:m, :], h0_rows[par][0:m, :],
                                   alpha[0:m, :].to_broadcast([m, F]), ALU.mult).then_inc(s_h0part, 1)
                pool.wait_ge(s_h0part, n + 1)
                if not isinstance(n, int) or n >= 2:
                    pool.wait_ge(s_z, n - 1)
                pool.tensor_tensor(xh[par][0:m, :], h0_part[0:m, :], at(xs, block(n), m), ALU.add)\
                    .then_inc(s_xh, 1)

            def inverse_std(n, par, m):
                pool.wait_ge(s_stats, n + 1)
                pool.wait_ge(s_rstd, n)
                pool.tensor_tensor(var_eps[0:m, :], mean_var[par][0:m, 1:2], ln_eps[0:m, :], ALU.add)\
                    .then_inc(s_vareps, 1)
                pool.wait_ge(s_vareps, n + 1)
                pool.tensor_tensor(rstd[par][0:m, :], var_eps[0:m, :], neg_half[0:m, :], ALU.pow)\
                    .then_inc(s_rstd, 1)

            def step(t, par, pair):
                odd = (par + 1) % 2
                if valid(t - 7):
                    m = rows_of(t - 7)
                    pool.wait_ge(s_rest, t - 6)
                    pool.tensor_tensor(at_cols(f_parts, block(t - 7), m, F, 2 * F), f_rest[0:m, :],
                                       low_scale[0:m, :].to_broadcast([m, F]), ALU.mult)\
                        .then_inc(s_flow, 1)
                if valid(t - 2):
                    residual(t - 2, par, pair - 1)
                if valid(t - 3):
                    inverse_std(t - 3, odd, rows_of(t - 3))
                if valid(t - 4):
                    m = rows_of(t - 4)
                    pool.wait_ge(s_xn, t - 3)
                    pool.tensor_copy(at(xs, block(t - 4), m), xn[par][0:m, :]).then_inc(s_kept, 1)
            pool.wait_ge(s_in["x"], 16)
            pool.wait_ge(s_in["xt"], 16)
            pool.wait_ge(s_xhigh, 1)
            for h, half in enumerate(X_HALF):
                if h > 0:
                    pool.wait_ge(s_xlow, h)
                pool.tensor_tensor(x_rest, xs[:, half, :].rearrange("p b f -> p (b f)"),
                                   x_parts[:, half, 0:F], ALU.subtract).then_inc(s_xrest, 1)
                pool.wait_ge(s_xrest, h + 1)
                pool.tensor_tensor(x_parts[:, half, F:2 * F], x_rest,
                                   low_scale.to_broadcast([P, NB // 2 * F]), ALU.mult).then_inc(s_xlow, 1)
            steps(pool, step, LAG)

            def step1(t, par, pair):
                if valid(t - 2):
                    inverse_std(t + (NB - 2), par, rows_of(t - 2))
            steps(pool, step1, 2)

        @engines.tensor
        def _(pe):
            pe.wait_ge(s_const, 10)
            pe.wait_ge(s_y, 1)
            for b in range(NB):
                if b >= 8 and b % 4 == 0:
                    pe.wait_ge(s_yt_sb, b // 4 - 1)
                m = rows_in(b)
                tr = pe.transpose(y_turned[b // 4 % 2][:, (b % 4) * P:(b % 4) * P + m], y2[0:m, b, :],
                                  ident_b[0:m, 0:m])
                if b % 4 == 3 or b == LAST:
                    tr.then_inc(s_yt, 1)
            pe.wait_ge(s_const, 10 + BITS)
            pe.wait_ge(s_y, 2)
            for b in range(NB):
                mm = pe.matmul(xnt_acc[0:2 * C, b * WORDS:(b + 1) * WORDS], y_halves[:, b, :],
                               pack[:, :], start=True, stop=True)
            mm.then_inc(s_yp, 1)
            pe.wait_ge(s_yp_sb, 1)

            def gram_words(part):
                for b in part:
                    if b >= 4:
                        pe.wait_ge(*gram_copied(b - 4))
                    k = rows_in(b)
                    pe.matmul(gram[b % 4][0:k, 0:NB * WORDS], y2_t[:, b * P:b * P + k], y_packed[:, :],
                              start=True, stop=True).then_inc(s_gram, 1)

            def pack_rows(t, par, m, h):
                pe.wait_ge(s_bits, t * 2 + h + 1)
                if h == 0 and (not isinstance(t, int) or t >= 2):
                    pe.wait_ge(s_words, t - 1)
                for b in range(h * HB, HB if h == 0 else NB):
                    k = rows_in(b)
                    c = b * P - HALF[h].start
                    mm = pe.matmul(words[par][0:k, b * WORDS:(b + 1) * WORDS],
                                   a_bits[h][0:m, c:c + k], pack[0:m, :], start=True, stop=True)
                mm.then_inc(s_packed, 1)

            def multiply_ready(n, par):
                pe.wait_ge(s_unpacked, n + 1)
                if not isinstance(n, int) or n >= 2:
                    pe.wait_ge(s_z, n - 1)

            def multiply_blocks(n, par, m, parts, blocks, first=False, last=False):
                for b in blocks:
                    k = rows_in(b)
                    mm = pe.matmul(acc[par][0:m, 0:PARTS],
                                   turned_at(n, par)[0:k, b, 0:m].bitcast(F16), parts[0:k, b, :],
                                   start=first and b == blocks[0], stop=last and b == blocks[-1])
                if last:
                    mm.then_inc(s_acc, 1)

            def multiply(n, par, m, parts, h):
                if h == 0:
                    multiply_ready(n, par)
                    if isinstance(n, int) and n == 0:
                        pe.wait_ge(s_xlow, 2)
                        pe.wait_ge(s_gram_act, len(GRAM_ACT))
                        pe.wait_ge(s_gram_dve, len(GRAM_DVE))
                multiply_blocks(n, par, m, parts, range(h * HB, HB if h == 0 else NB), h == 0, h == 1)

            def early(t, lo, hi):
                if lo == 0:
                    multiply_ready(t + NB, t)
                    pe.wait_ge(s_cleared, 3)
                    pe.wait_ge(s_flow, EARLY)
                multiply_blocks(t + NB, t, rows_of(t), f_parts, [block(u) for u in range(lo, hi)], lo == 0)

            def step(t, par, pair):
                odd = (par + 1) % 2
                if valid(t):
                    pack_rows(t, par, rows_of(t), 0)
                if valid(t - 5):
                    m5 = rows_of(t - 5)
                    pe.wait_ge(s_xn, t - 4)
                    pe.transpose(xnt_acc[:, 0:m5], xn[odd][0:m5, :], ident[0:m5, 0:m5]).then_inc(s_xnt, 1)
                if valid(t - 2):
                    multiply(t - 2, par, rows_of(t - 2), x_parts, 0)
                if valid(t - 6):
                    m6 = rows_of(t - 6)
                    pe.wait_ge(s_in["wg"], 16)
                    pe.wait_ge(s_bias_sb, 1)
                    pe.wait_ge(s_h2, t - 5)
                    if not isinstance(t, int) or t >= 7:
                        pe.wait_ge(s_rest, t - 6)
                    pe.matmul(feat_acc[0:m6, 0:F], h2_t[:, 0:m6], wg[:, :], start=True, stop=True)\
                        .then_inc(s_feat, 1)
                if isinstance(t, int) and t == NB + 4:
                    early(1, 0, CUT[0])
                if isinstance(t, int) and t == LAST:
                    multiply(t - 2, par, rows_of(t - 2), x_parts, 1)
                if valid(t):
                    pack_rows(t, par, rows_of(t), 1)
                if valid(t - 5):
                    pe.wait_ge(s_in["wp"], 16)
                    pe.wait_ge(s_xnt_sb, t - 4)
                    if not isinstance(t, int) or t >= 6:
                        pe.wait_ge(s_h2, t - 5)
                    pe.matmul(proj_acc[:, 0:m5], wp[:, :], xn_t[:, 0:m5], start=True, stop=True)\
                        .then_inc(s_proj, 1)
                if valid(t - 2) and not (isinstance(t, int) and t == LAST):
                    multiply(t - 2, par, rows_of(t - 2), x_parts, 1)
                if isinstance(t, int) and t == NB + 2:
                    early(0, 0, EARLY // 2)
                if isinstance(t, int) and t == NB + 3:
                    early(0, EARLY // 2, EARLY)
                if isinstance(t, int) and t == NB + 4:
                    early(1, CUT[0], CUT[1])
                if isinstance(t, int) and t == NB + 5:
                    early(1, CUT[1], CUT[2])

            def bias():
                pe.wait_ge(s_in["bg"], 16)
                pe.matmul(feat_acc[:, 0:F], ones[0:1, :], bg_row[:, :], start=True, stop=True)\
                    .then_inc(s_bias, 1)
            steps(pe, step, LAG, {0: lambda: gram_words(GRAM[0]), 1: lambda: gram_words(GRAM[1]), 2: bias})
            pe.wait_ge(s_flow, NB)

            def step1(t, par, pair):
                if isinstance(t, int) and t < 2:
                    if t == 1:
                        early(1, CUT[2], EARLY)
                    multiply_blocks(t + NB, par, rows_of(t), f_parts,
                                    [block(u) for u in range(EARLY, NB)], last=True)
                    return
                for h in range(2):
                    multiply(t + NB, par, rows_of(t), f_parts, h)
            steps(pe, step1, 0)
            pe.wait_ge(s_good, CHECKS)
            pe.matmul(feat_acc[0:1, 0:1], good[:, :], ones[:, 0:1], start=True, stop=True)\
                .then_inc(s_sum, 1)

        @engines.scalar
        def _(act):
            act.wait_ge(s_const, 8)
            act.activation(tanh1, ones[:, 0:1], ACT.Tanh).then_inc(s_tanh1, 1)
            act.wait_ge(s_cleared, 2)

            def gram_copies(part):
                for b in part:
                    if b in GRAM_ACT:
                        copy_gram(lambda o, i: act.activation(o, i, ACT.Copy), act, b)

            def high_parts():
                act.wait_ge(s_in["x"], 16)
                act.wait_ge(s_in["xt"], 16)
                act.activation(x_parts[:, :, 0:F], xs[:, :, :], ACT.Copy).then_inc(s_xhigh, 1)
                gram_copies(GRAM[0])

            def count_zeros(t, par, pair, h, m):
                act.wait_ge(s_rows[par][h], pair * 16 + 16)
                w = HALF[h].stop - HALF[h].start
                col = zeros_in[0:m, bass.ds(t * 2 + h, 1)]
                act.wait_ge(s_counted, t * 2 + h)
                act.activation(count_out[0:m, 0:w], a_rows[par][h][0:m, 0:w], ACT.Relu,
                               bias=ones[0:m, 0:1], scale=-HUGE,
                               accum_out=col).then_inc(s_counted, 1)

            def measure(parts, sums, t, n):
                m = rows_of(t)
                if not isinstance(n, int) or n >= 1:
                    act.wait_ge(s_measured, n)
                if isinstance(n, int) and n == 0:
                    act.wait_ge(s_xhigh, 1)
                act.activation(square_out[0:m, :], at_cols(parts, block(t), m, 0, F), ACT.Square,
                               scale=1.0 / PART_MAX, accum_out=sums[0:m, bass.ds(t, 1)])\
                    .then_inc(s_measured, 1)

            def step(t, par, pair):
                odd = (par + 1) % 2
                if valid(t - 1):
                    act.wait_ge(s_packed, t * 2)
                    act.activation(at(a_words, block(t - 1), P), words[odd][:, 0:NB * WORDS], ACT.Copy)\
                        .then_inc(s_words, 1)
                if valid(t - 6):
                    m6 = rows_of(t - 6)
                    act.wait_ge(s_in["bp"], 16)
                    act.wait_ge(s_proj, t - 5)
                    if not isinstance(t, int) or t >= 7:
                        act.wait_ge(s_feat, t - 6)
                    act.activation(h2_t[:, 0:m6], proj_acc[:, 0:m6], ACT.Tanh, bias=bp_col[:, :])\
                        .then_inc(s_h2, 1)
                if valid(t):
                    count_zeros(t, par, pair, 0, rows_of(t))
                if valid(t - 5):
                    m5 = rows_of(t - 5)
                    act.wait_ge(s_xnt, t - 4)
                    if not isinstance(t, int) or t >= 6:
                        act.wait_ge(s_proj, t - 5)
                    act.activation(xn_t[:, 0:m5], xnt_acc[:, 0:m5], ACT.Copy).then_inc(s_xnt_sb, 1)
                if valid(t):
                    count_zeros(t, par, pair, 1, rows_of(t))
                if valid(t - 1):
                    measure(x_parts, x_sums, t - 1, t - 1)
                if valid(t - 6):
                    act.wait_ge(s_feat, t - 5)
                    act.activation(at_cols(f_parts, block(t - 6), m6, 0, F), feat_acc[0:m6, 0:F], ACT.Copy)\
                        .then_inc(s_high, 1)
            steps(act, step, LAG, {0: high_parts, 1: lambda: gram_copies(GRAM[1])})
            act.wait_ge(s_high, NB)
            steps(act, lambda t, par, pair: measure(f_parts, f_sums, t, t + NB), 0)

        @engines.vector
        def _(dve):
            dve.memset(y_nat[:, FULL, :], 0.0)
            dve.memset(xs[:, FULL, :], 0.0).then_inc(s_cleared, 1)
            for p in range(2):
                dve.memset(words[p][:, LAST * WORDS:NB * WORDS], 0.0)
            dve.memset(g_words[:, :, LAST * WORDS:NB * WORDS], 0)
            dve.memset(zeros_in[:, :], N / 2)
            for a in (degree, x_sums, f_sums):
                dve.memset(a[:, :], 0.0)
            dve.memset(x_parts[:, :, 2 * F], 1.0)
            dve.memset(x_parts[:, :, 2 * F + 1], LOW)
            dve.memset(y_halves, 0.0).then_inc(s_cleared, 1)
            dve.wait_ge(s_in["y"], 16)
            dve.wait_ge(s_in["yt"], 16)
            dve.wait_ge(s_cleared, 2)
            dve.tensor_copy(y2[:, :, 0:C], y_nat[:, :, :])
            dve.tensor_copy(y2[:, :, C:2 * C], y_nat[:, :, :]).then_inc(s_y, 1)
            dve.tensor_copy(y_halves[0:P // 2, :, 0:C], y_nat[0:P // 2, :, :])
            dve.tensor_copy(y_halves[P // 2:P, :, C:2 * C], y_nat[P // 2:P, :, :]).then_inc(s_y, 1)
            for g in range(-(-NB // 4)):
                dve.wait_ge(s_yt, g + 1)
                w = min((g + 1) * 4 * P, N) - g * 4 * P
                dve.tensor_copy(y2_t[:, g * 4 * P:g * 4 * P + w],
                                y_turned[g % 2][:, 0:w]).then_inc(s_yt_sb, 1)
            dve.wait_ge(s_yp, 1)
            dve.tensor_copy(y_packed[:, :], xnt_acc[0:2 * C, 0:NB * WORDS]).then_inc(s_yp_sb, 1)

            def gram_copies(part):
                for b in part:
                    if b in GRAM_DVE:
                        copy_gram(dve.tensor_copy, dve, b)

            def bias():
                dve.wait_ge(s_bias, 1)
                dve.tensor_copy(bg_all[:, :], feat_acc[:, 0:F]).then_inc(s_bias_sb, 1)

            def feature_ones():
                dve.memset(f_parts[:, :, 2 * F], 1.0)
                dve.memset(f_parts[:, :, 2 * F + 1], LOW).then_inc(s_cleared, 1)

            k = [0]

            def done(ins):
                k[0] += 1
                ins.then_inc(s_good, 1)
                dve.wait_ge(s_good, k[0])

            def check_y_sums():
                done(dve.tensor_reduce(chk[:, :], y_nat[:, :, :], AX.X, ALU.add))
                done(dve.tensor_scalar(holds[:, 1, :], chk[:, :], 1.0, None, ALU.is_le))

            def check_y():
                y_flat = y_nat[:, :, :].rearrange("p b c -> p (b c)")
                done(dve.scalar_tensor_tensor(y_flat, y_flat, 1.0, y_flat, ALU.is_equal, ALU.is_equal))
                done(dve.tensor_reduce(holds[:, 2, :], y_nat[:, :, :], AX.X, ALU.min))

            def check_sums():
                dve.wait_ge(s_measured, 2 * NB)
                done(dve.tensor_scalar(holds[:, 3, :], x_sums[:, :], 1.0, None, ALU.is_le))
                done(dve.tensor_scalar(holds[:, 4, :], f_sums[:, :], 1.0, None, ALU.is_le))
                dve.wait_ge(s_counted, 2 * NB)
                zeros_in_2 = zeros_in[:, :].rearrange("p (b h) -> p b h", h=2)
                done(dve.tensor_tensor(chk[:, :], zeros_in_2[:, :, 0], zeros_in_2[:, :, 1], ALU.add))
                done(dve.tensor_scalar(need[:, :], chk[:, :], -1.0, float(N), ALU.mult, ALU.add))
                done(dve.tensor_scalar(holds[:, 5, :], need[:, :], float(TOPK), None, ALU.is_le))
                assert k[0] == CHECKS - 2

            def unpack(n, par, m, source, lo, hi):
                if isinstance(n, int) and n == 1 and lo == 0:
                    dve.wait_ge(s_xlow, 2)
                if isinstance(n, int) and n == NB + 2:
                    if lo == 0:
                        dve.wait_ge(s_bits, 2 * NB)
                        dve.wait_ge(s_counted, 2 * NB)
                elif lo == 0 and (not isinstance(n, int) or n >= 2):
                    dve.wait_ge(s_acc, n - 1)
                last = BITS if m == P else 1
                for bit in range(lo, min(hi, last)):
                    shift = ONE_BIT - bit
                    op = ALU.logical_shift_left if shift >= 0 else ALU.logical_shift_right
                    up = dve.tensor_scalar(
                        turned_at(n, par)[:, :, bit * WORDS:(bit + 1) * WORDS],
                        source.rearrange("p (b w) -> p b w", w=WORDS),
                        abs(shift), 1 << ONE_BIT, op, ALU.bitwise_and)
                    if bit == last - 1:
                        up.then_inc(s_unpacked, 1)

            def cast(t, par, pair, h):
                m = rows_of(t)
                w = HALF[h].stop - HALF[h].start
                dve.wait_ge(s_rows[par][h], pair * 16 + 16)
                if not isinstance(t, int) or t >= 1:
                    dve.wait_ge(s_packed, t * 2 - 1 + h)
                dve.tensor_scalar(a_bits[h][0:m, 0:w], a_rows[par][h][0:m, 0:w], 1.0, None,
                                  ALU.is_equal).then_inc(s_bits, 1)

            def normalize(n, par, m):
                dve.wait_ge(s_rstd, n + 1)
                return dve.tensor_scalar(xn[par][0:m, :], z[par][0:m, :], mean_var[par][0:m, 0:1],
                                         rstd[par][0:m, :], ALU.subtract, ALU.mult)

            def step(t, par, pair):
                odd = (par + 1) % 2
                if valid(t):
                    cast(t, par, pair, 0)
                if valid(t - 7):
                    m7 = rows_of(t - 7)
                    dve.wait_ge(s_high, t - 6)
                    if not isinstance(t, int) or t >= 8:
                        dve.wait_ge(s_flow, t - 7)
                    dve.tensor_tensor(f_rest[0:m7, :], feat_acc[0:m7, 0:F],
                                      at_cols(f_parts, block(t - 7), m7, 0, F),
                                      ALU.subtract).then_inc(s_rest, 1)

                def bits(lo, hi):
                    if valid(t - 1):
                        unpack(t - 1, odd, rows_of(t - 1), same_class[:, :], lo, hi)


                def begin(t_of, u, lo, hi):
                    if isinstance(t, int) and t == t_of:
                        unpack(u + NB, u % 2, rows_of(u), at(a_words, block(u), P), lo, hi)

                begin(NB + 3, 1, 0, BITS // 2)
                if valid(t - 1):
                    if isinstance(t, int) and t == 1:
                        cast(t, par, pair, 1)
                        gram_copies(GRAM[1])
                        dve.wait_ge(s_gram_dve, len(GRAM_DVE))
                        dve.wait_ge(s_gram_act, len(GRAM_ACT))
                    dve.wait_ge(s_words, t)
                    dve.wait_ge(s_unpacked, t - 1)
                    dve.tensor_tensor(same_class[:, :], at(a_words, block(t - 1), P),
                                      at(g_words, block(t - 1), P), ALU.bitwise_and).then_inc(s_masked, 1)
                if valid(t - 4):
                    m4 = rows_of(t - 4)
                    if not isinstance(t, int) or t >= 6:
                        dve.wait_ge(s_xnt, t - 5)
                        dve.wait_ge(s_kept, t - 5)
                    normalize(t - 4, par, m4).then_inc(s_xn, 1)
                if valid(t - 1):
                    dve.wait_ge(s_masked, t)
                bits(0, 2)
                post = valid(t - 3)
                if post:
                    m = rows_of(t - 3)
                    dve.wait_ge(s_acc, t - 2)
                    dve.wait_ge(s_z, t - 3)
                    dve.tensor_scalar(rs[0:m, 0:2], acc[odd][0:m, 2 * F:2 * F + 2], 2 * L1_EPS,
                                      1 / (1 - ALPHA), ALU.max, ALU.mult).then_inc(s_floor, 1)
                bits(2, 4)
                if post:
                    dve.wait_ge(s_floor, t - 2)
                    dve.reciprocal(rs[0:m, 2:4], rs[0:m, 0:2]).then_inc(s_inverse, 1)
                bits(4, 6)
                if post:
                    dve.wait_ge(s_inverse, t - 2)
                    dve.wait_ge(s_xh, t - 2)
                    dve.scalar_tensor_tensor(z_high[0:m, :], acc[odd][0:m, 0:F], rs[0:m, 2:3],
                                             xh[odd][0:m, :], ALU.mult, ALU.add).then_inc(s_zhigh, 1)
                bits(6, 8)
                if post:
                    dve.wait_ge(s_zhigh, t - 2)
                    if not isinstance(t, int) or t >= 5:
                        dve.wait_ge(s_xn, t - 4)
                    dve.scalar_tensor_tensor(z[odd][0:m, :], acc[odd][0:m, F:2 * F], rs[0:m, 3:4],
                                             z_high[0:m, :], ALU.mult, ALU.add).then_inc(s_z, 1)
                if valid(t) and not (isinstance(t, int) and t == 1):
                    cast(t, par, pair, 1)
                if post:
                    dve.wait_ge(s_z, t - 2)
                    dve.wait_ge(s_stats, t - 3)
                    dve.bn_stats(stats[0:m, :], z[odd][0:m, :]).then_inc(s_bn, 1)
                bits(8, 10)
                if post:
                    dve.wait_ge(s_bn, t - 2)
                    dve.sem_inc(s_passed, 1)
                    dve.bn_aggr(mean_var[odd][0:m, :], stats[0:m, :]).then_inc(s_stats, 1)
                bits(10, BITS)
                begin(NB + 1, 0, 0, BITS)
                begin(NB + 3, 1, BITS // 2, BITS)
                begin(NB + 4, 2, 0, BITS)

            steps(dve, step, LAG, {0: lambda: gram_copies(GRAM[0]), 1: feature_ones, 3: bias, LAG: check_y_sums})

            dve.wait_ge(s_tanh1, 1)
            dve.tensor_scalar(half_tanh1, tanh1, 0.5, None, ALU.mult).then_inc(s_half, 1)
            dve.tensor_scalar(low_tanh1, tanh1, 0.5 / LOW, None, ALU.mult).then_inc(s_half, 1)
            dve.wait_ge(s_half, 2)
            dve.wait_ge(s_bias_sb, 1)
            dve.wait_ge(s_kept, NB)
            dve.wait_ge(s_xnt, NB)

            def step1(t, par, pair):
                odd = (par + 1) % 2

                def bits(lo, hi):
                    if valid(t) and (not isinstance(t, int) or t > 2):
                        unpack(t + NB, par, rows_of(t), at(a_words, block(t), P), lo, hi)

                bits(0, 2)
                post = valid(t - 2)
                if post:
                    m = rows_of(t - 2)
                    dve.wait_ge(s_acc, t + (NB - 1))
                    dve.wait_ge(s_biased, t - 2)
                    dve.scalar_tensor_tensor(low_feat[0:m, :], acc[par][0:m, F:2 * F], low_tanh1[0:m, :],
                                             bg_all[0:m, :], ALU.mult, ALU.add).then_inc(s_lowfeat, 1)
                    dve.tensor_scalar(degree[0:m, bass.ds(t - 2, 1)], acc[par][0:m, 2 * F:2 * F + 1], 0.5,
                                      None, ALU.mult).then_inc(s_degree, 1)
                bits(2, 4)
                if post:
                    dve.wait_ge(s_lowfeat, t - 1)
                    dve.wait_ge(s_z, t + (NB - 2))
                    dve.scalar_tensor_tensor(feat[0:m, :], acc[par][0:m, 0:F], half_tanh1[0:m, :],
                                             low_feat[0:m, :], ALU.mult, ALU.add).then_inc(s_biased, 1)
                bits(4, 6)
                if post:
                    dve.wait_ge(s_biased, t - 1)
                    dve.wait_ge(s_degree, t - 1)
                    if not isinstance(t, int) or t >= 4:
                        dve.wait_ge(s_result, t - 3)
                    dve.scalar_tensor_tensor(z[par][0:m, :], feat[0:m, :], 0.0, at(xs, block(t - 2), m),
                                             ALU.max, ALU.add).then_inc(s_z, 1)
                bits(6, 8)
                if post:
                    dve.wait_ge(s_z, t + (NB - 1))
                    dve.wait_ge(s_stats, t + (NB - 2))
                    dve.bn_stats(stats[0:m, :], z[par][0:m, :]).then_inc(s_bn, 1)
                bits(8, 10)
                if post:
                    dve.wait_ge(s_bn, t + (NB - 1))
                    dve.sem_inc(s_passed, 1)
                    dve.bn_aggr(mean_var[par][0:m, :], stats[0:m, :]).then_inc(s_stats, 1)
                bits(10, 14)
                if valid(t - 3):
                    if not isinstance(t, int) or t >= 5:
                        dve.wait_ge(s_out[odd], (pair - 2 + par) * 16)
                    normalize(t + (NB - 3), odd, rows_of(t - 3)).then_inc(s_result, 1)
                bits(14, BITS)
                if isinstance(t, int) and t == 1:
                    check_y()
                if isinstance(t, int) and t == NB - 1:
                    check_sums()
            steps(dve, step1, 3)

            dve.wait_ge(s_degree, NB)
            done(dve.tensor_tensor(holds[:, 0, :], degree[:, :], need[:, :], ALU.is_equal))
            done(dve.tensor_reduce(good[:, :], holds[:, :, :], AX.XY, ALU.min))
            dve.wait_ge(s_sum, 1)
            dve.tensor_scalar(flag[:, :], feat_acc[0:1, 0:1], float(P), None, ALU.not_equal)\
                .then_inc(s_flag, 1)


def general_path(nc, x, adj, h0, y, w_proj, b_proj, w_gcn, b_gcn, out, flag):
    N, F = x.shape
    C = y.shape[1]
    FULL = N // P
    TAIL = N - FULL * P
    NB = FULL + 1
    NG = -(-NB // GROUP)
    assert F == P and 0 < TAIL <= 32

    def rows_of(b):
        return P if b < FULL else TAIL

    def blocks_of(g):
        return range(g * GROUP, min((g + 1) * GROUP, NB))

    def cols_of(g):
        return slice(g * GROUP * P, min((g + 1) * GROUP * P, N))

    with ExitStack() as ctx:
        def sb(name, shape, dt=F32):
            return ctx.enter_context(nc.sbuf_tensor(f"general_{name}", shape, dt))

        def ps(name, shape, dt=F32):
            return ctx.enter_context(nc.psum_tensor(f"general_{name}", shape, dt))

        def sem(name):
            return ctx.enter_context(nc.semaphore(f"general_{name}"))

        ident = sb("ident", [P, P])
        ones = sb("ones", [1, P])
        neg_half = sb("neg_half", [P, 1])
        wp = sb("wp", [F, F])
        wg = sb("wg", [F, F])
        bp_col = sb("bp_col", [F, 1])
        bg_row = sb("bg_row", [1, F])
        bg_all = sb("bg_all", [P, F])
        y_nat = sb("y_nat", [P, NB, C])
        y_t = sb("y_t", [C, N])
        xs = sb("xs", [P, NB, F])
        h0s = sb("h0s", [P, NB, F])
        x1 = sb("x1", [P, NB, F])
        feats = sb("feats", [P, NB, F])
        a_rows = sb("a_rows", [P, N])
        weights = sb("weights", [P, N])
        scratch = sb("scratch", [P, N])
        weights_t = sb("weights_t", [P, NB, P])
        y_block = sb("y_block", [C, P])
        col = sb("col", [P, 16])
        icol = sb("icol", [P, 8], I32)
        stats = sb("stats", [P, 8])
        z = sb("z", [P, F])
        z1 = sb("z1", [P, F])
        xn = sb("xn", [P, F])
        xn_t = sb("xn_t", [F, P])
        h2_t = sb("h2_t", [F, P])
        result = sb("result", [P, F])

        gram = [ps(f"gram{i}", [P, GROUP * P]) for i in range(2)]
        turned = [ps(f"turned{i}", [P, GROUP, P]) for i in range(2)]
        support = ps("support", [P, F])
        small = ps("small", [P, GROUP, P])

        s_const = sem("s_const")
        s_in = [sem(f"s_in{i}") for i in range(9)]
        s_setup_pe = sem("s_setup_pe")
        s_setup_dve = sem("s_setup_dve")
        s_dve = sem("s_dve")
        s_passed = sem("s_passed")
        s_rows = sem("s_rows")
        s_rows_free = sem("s_rows_free")
        s_yblock = sem("s_yblock")
        s_gram = sem("s_gram")
        s_gram_free = sem("s_gram_free")
        s_weighted = sem("s_weighted")
        s_rowsum = sem("s_rowsum")
        s_scaled = sem("s_scaled")
        s_turned = sem("s_turned")
        s_copied = sem("s_copied")
        s_support = sem("s_support")
        s_var = sem("s_var")
        s_rstd = sem("s_rstd")
        s_xn = sem("s_xn")
        s_xnt = sem("s_xnt")
        s_xnt_sb = sem("s_xnt_sb")
        s_proj = sem("s_proj")
        s_h2 = sem("s_h2")
        s_feat = sem("s_feat")
        s_feat_sb = sem("s_feat_sb")
        s_tanh = sem("s_tanh")
        s_result = sem("s_result")
        s_out = sem("s_out")

        def block_view(a):
            return a[0:FULL * P, :].rearrange("(b p) f -> p b f", p=P)

        block = ctx.enter_context(nc.Block())

        def row_range(t, m):
            return bass.ds(t * P, m)

        @block.sync
        def _(sp):
            bad = sp.value_load(flag[0:1, 0:1], min_val=0, max_val=1)
            with sp.If(bad != 0):
                sp.dma_start(y_nat[:, 0:FULL, :], block_view(y)).then_inc(s_in[0], 16)
                sp.dma_start(y_nat[0:TAIL, FULL, :], y[FULL * P:N, :]).then_inc(s_in[1], 16)
                sp.dma_start(xs[:, 0:FULL, :], block_view(x)).then_inc(s_in[2], 16)
                sp.dma_start(xs[0:TAIL, FULL, :], x[FULL * P:N, :]).then_inc(s_in[3], 16)
                sp.dma_start(h0s[:, 0:FULL, :], block_view(h0)).then_inc(s_in[4], 16)
                sp.dma_start(h0s[0:TAIL, FULL, :], h0[FULL * P:N, :]).then_inc(s_in[5], 16)
                sp.dma_start(wp[:, :], w_proj).then_inc(s_in[6], 16)
                sp.dma_start(wg[:, :], w_gcn).then_inc(s_in[7], 16)
                sp.dma_start(bp_col[:, :], b_proj.rearrange("(p a) -> p a", a=1)).then_inc(s_in[8], 16)
                sp.dma_start(bg_row[:, :], b_gcn.rearrange("(a p) -> a p", a=1)).then_inc(s_in[8], 16)

                def load(t, s, m):
                    sp.wait_ge(s_rows_free, s)
                    sp.dma_start(a_rows[0:m, :], adj[row_range(t, m), :]).then_inc(s_rows, 16)

                def store(t, m):
                    sp.wait_ge(s_result, t + 1)
                    sp.dma_start(out[row_range(t, m), :], result[0:m, :]).then_inc(s_out, 16)

                sp.sem_inc(s_out, 16)
                load(0, 0, P)
                with sp.Fori(1, FULL) as t:
                    load(t, t, P)
                load(FULL, FULL, TAIL)
                with sp.Fori(0, FULL) as t:
                    load(t, t + NB, P)
                    store(t, P)
                load(FULL, FULL + NB, TAIL)
                store(FULL, TAIL)
                sp.wait_ge(s_out, 16 * (NB + 1))

        @block.gpsimd
        def _(pool):
            bad = pool.value_load(flag[0:1, 0:1], min_val=0, max_val=1)
            with pool.If(bad != 0):
                pool.memset(ident[:, :], 0.0).then_inc(s_const, 1)
                pool.memset(ones[:, :], 1.0).then_inc(s_const, 1)
                pool.memset(neg_half[:, :], -0.5).then_inc(s_const, 1)
                pool.wait_ge(s_const, 3)
                pool.affine_select(out=ident[:, :], in_=ident[:, :], compare_op=ALU.not_equal, fill=1.0,
                                   base=0, pattern=[[-1, P]], channel_multiplier=1).then_inc(s_const, 1)

                def rstd(s, m):
                    pool.wait_ge(s_var, s + 1)
                    pool.tensor_tensor(col[0:m, 5:6], col[0:m, 4:5], neg_half[0:m, :], ALU.pow)\
                        .then_inc(s_rstd, 1)

                for first in (0, NB):
                    with pool.Fori(first, first + FULL) as s:
                        rstd(s, P)
                    rstd(first + FULL, TAIL)

        @block.tensor
        def _(pe):
            bad = pe.value_load(flag[0:1, 0:1], min_val=0, max_val=1)
            with pe.If(bad != 0):
                pe.wait_ge(s_const, 4)
                pe.wait_ge(s_in[0], 16)
                pe.wait_ge(s_in[1], 16)
                for g in range(NG):
                    if g:
                        pe.wait_ge(s_setup_dve, g)
                    for b in blocks_of(g):
                        m = rows_of(b)
                        mm = pe.transpose(small[0:C, b % GROUP, 0:m], y_nat[0:m, b, :], ident[0:m, 0:m])
                    mm.then_inc(s_setup_pe, 1)
                pe.wait_ge(s_in[8], 32)
                pe.wait_ge(s_setup_dve, NG)
                pe.matmul(small[:, 0, :], ones[:, :], bg_row[:, :], start=True, stop=True)\
                    .then_inc(s_setup_pe, 1)
                pe.wait_ge(s_setup_dve, NG + 1)
                for i in (2, 3, 6, 7):
                    pe.wait_ge(s_in[i], 16)

                def gram_rows(t, m):
                    pe.wait_ge(s_yblock, t + 1)
                    for g in range(NG):
                        c = cols_of(g)
                        pe.wait_ge(s_gram_free, t * NG + (g + 1))
                        pe.matmul(gram[g % 2][0:m, 0:c.stop - c.start], y_block[:, 0:m], y_t[:, c],
                                  start=True, stop=True).then_inc(s_gram, 1)

                def product(s, m, rhs):
                    pe.wait_ge(s_scaled, s + 1)
                    for g in range(NG):
                        pe.wait_ge(s_copied, s * NG + (g + 1))
                        for b in blocks_of(g):
                            k = rows_of(b)
                            mm = pe.transpose(turned[g % 2][0:k, b % GROUP, 0:m],
                                              weights[0:m, b * P:b * P + k], ident[0:m, 0:m])
                        mm.then_inc(s_turned, 1)
                    pe.wait_ge(s_copied, s * NG + (NG + 2))
                    for b in range(NB):
                        k = rows_of(b)
                        mm = pe.matmul(support[0:m, :], weights_t[0:k, b, 0:m], rhs[0:k, b, :],
                                       start=(b == 0), stop=(b == NB - 1))
                    mm.then_inc(s_support, 1)

                def layer0(t, m):
                    gram_rows(t, m)
                    product(t, m, xs)
                    pe.wait_ge(s_xn, t + 1)
                    pe.transpose(small[:, 0, 0:m], xn[0:m, :], ident[0:m, 0:m]).then_inc(s_xnt, 1)
                    pe.wait_ge(s_xnt_sb, t + 1)
                    pe.matmul(small[:, 1, 0:m], wp[:, :], xn_t[:, 0:m], start=True, stop=True)\
                        .then_inc(s_proj, 1)
                    pe.wait_ge(s_h2, t + 1)
                    pe.matmul(small[0:m, 2, :], h2_t[:, 0:m], wg[:, :], start=True, stop=True)\
                        .then_inc(s_feat, 1)

                with pe.Fori(0, FULL) as t:
                    layer0(t, P)
                layer0(FULL, TAIL)
                pe.wait_ge(s_feat_sb, NB)
                with pe.Fori(0, FULL) as t:
                    product(t + NB, P, feats)
                product(FULL + NB, TAIL, feats)

        @block.scalar
        def _(act):
            bad = act.value_load(flag[0:1, 0:1], min_val=0, max_val=1)
            with act.If(bad != 0):
                def copy_turned(s, m):
                    act.wait_ge(s_support, s)
                    for g in range(NG):
                        act.wait_ge(s_turned, s * NG + (g + 1))
                        whole = [b for b in blocks_of(g) if b < FULL]
                        if whole:
                            cp = act.activation(weights_t[:, whole[0]:whole[-1] + 1, 0:m],
                                                turned[g % 2][:, 0:len(whole), 0:m], ACT.Copy)
                        if NB - 1 in blocks_of(g):
                            cp = act.activation(weights_t[0:TAIL, FULL, 0:m],
                                                turned[g % 2][0:TAIL, FULL % GROUP, 0:m], ACT.Copy)
                        cp.then_inc(s_copied, 1)

                def layer0(t, m):
                    act.wait_ge(s_weighted, t + 1)
                    act.activation(a_rows[0:m, :], weights[0:m, :], ACT.Abs, accum_out=col[0:m, 0:1])\
                        .then_inc(s_rowsum, 1)
                    copy_turned(t, m)
                    act.wait_ge(s_xnt, t + 1)
                    act.activation(xn_t[:, 0:m], small[:, 0, 0:m], ACT.Copy).then_inc(s_xnt_sb, 1)
                    act.wait_ge(s_proj, t + 1)
                    act.activation(h2_t[:, 0:m], small[:, 1, 0:m], ACT.Tanh, bias=bp_col[:, :])\
                        .then_inc(s_h2, 1)

                def layer1(t, m):
                    act.wait_ge(s_rows, t * 16 + 16 * (NB + 1))
                    act.wait_ge(s_support, t + NB)
                    act.activation(weights[0:m, :], a_rows[0:m, :], ACT.Square).then_inc(s_tanh, 1)
                    act.wait_ge(s_tanh, t * 2 + 1)
                    act.activation(weights[0:m, :], weights[0:m, :], ACT.Tanh).then_inc(s_tanh, 1)
                    copy_turned(t + NB, m)

                act.wait_ge(s_in[8], 32)
                layer0(0, P)
                with act.Fori(1, FULL) as t:
                    layer0(t, P)
                layer0(FULL, TAIL)
                with act.Fori(0, FULL) as t:
                    layer1(t, P)
                layer1(FULL, TAIL)

        @block.vector
        def _(dve):
            bad = dve.value_load(flag[0:1, 0:1], min_val=0, max_val=1)
            with dve.If(bad != 0):
                base = [0, 0]

                def done(ins):
                    base[1] += 1
                    ins.then_inc(s_dve, 1)
                    dve.wait_ge(s_dve, base[0] + base[1])

                for g in range(NG):
                    dve.wait_ge(s_setup_pe, g + 1)
                    whole = [b for b in blocks_of(g) if b < FULL]
                    if whole:
                        cp = dve.tensor_copy(y_t[:, whole[0] * P:(whole[-1] + 1) * P],
                                             small[0:C, 0:len(whole), :].rearrange("c b p -> c (b p)"))
                    if NB - 1 in blocks_of(g):
                        cp = dve.tensor_copy(y_t[:, FULL * P:N], small[0:C, FULL % GROUP, 0:TAIL])
                    cp.then_inc(s_setup_dve, 1)
                dve.wait_ge(s_setup_pe, NG + 1)
                dve.tensor_copy(bg_all[:, :], small[:, 0, :]).then_inc(s_setup_dve, 1)
                dve.wait_ge(s_setup_dve, NG + 1)
                for i in range(2, 6):
                    dve.wait_ge(s_in[i], 16)
                dve.sem_inc(s_gram_free, 2)
                dve.sem_inc(s_copied, 2)

                def layer_norm(s, m, zin, zout):
                    done(dve.bn_stats(stats[0:m, 0:6], zin[0:m, :]))
                    dve.sem_inc(s_passed, 1)
                    done(dve.bn_aggr(col[0:m, 2:4], stats[0:m, 0:6]))
                    dve.tensor_scalar(col[0:m, 4:5], col[0:m, 3:4], LN_EPS, None, ALU.add)\
                        .then_inc(s_var, 1)
                    dve.wait_ge(s_rstd, s + 1)
                    return dve.tensor_scalar(zout[0:m, :], zin[0:m, :], col[0:m, 2:3], col[0:m, 5:6],
                                             ALU.subtract, ALU.mult)

                def at(a, t, m):
                    if isinstance(t, int):
                        return a[0:m, t, :]
                    return a[0:m, bass.ds(t, 1), :].rearrange("p a f -> p (a f)")

                def layer0(t, m):
                    base[:] = [t * STEPS0, 0]
                    dve.tensor_copy(y_block[:, 0:m], y_t[:, row_range(t, m)]).then_inc(s_yblock, 1)
                    dve.wait_ge(s_rows, t * 16 + 16)
                    for g in range(NG):
                        c = cols_of(g)
                        dve.wait_ge(s_gram, t * NG + (g + 1))
                        dve.tensor_tensor(weights[0:m, c], gram[g % 2][0:m, 0:c.stop - c.start],
                                          a_rows[0:m, c], ALU.mult).then_inc(s_gram_free, 1)
                    dve.wait_ge(s_gram_free, t * NG + (NG + 2))
                    dve.sem_inc(s_weighted, 1)
                    dve.wait_ge(s_rowsum, t + 1)
                    done(dve.tensor_scalar(col[0:m, 1:2], col[0:m, 0:1], L1_EPS, None, ALU.max))
                    done(dve.reciprocal(col[0:m, 1:2], col[0:m, 1:2]))
                    done(dve.tensor_scalar(weights[0:m, :], weights[0:m, :], col[0:m, 1:2], None, ALU.mult))
                    dve.sem_inc(s_scaled, 1)
                    dve.sem_inc(s_rows_free, 1)
                    done(dve.scalar_tensor_tensor(z1[0:m, :], at(h0s, t, m), ALPHA, at(xs, t, m),
                                                  ALU.mult, ALU.add))
                    dve.wait_ge(s_support, t + 1)
                    done(dve.scalar_tensor_tensor(z[0:m, :], support[0:m, :], 1.0 - ALPHA, z1[0:m, :],
                                                  ALU.mult, ALU.add))
                    layer_norm(t, m, z, xn).then_inc(s_xn, 1)
                    dve.wait_ge(s_xn, t + 1)
                    done(dve.tensor_copy(at(x1, t, m), xn[0:m, :]))
                    dve.wait_ge(s_feat, t + 1)
                    dve.tensor_copy(at(feats, t, m), small[0:m, 2, :]).then_inc(s_feat_sb, 1)
                    assert base[1] == STEPS0

                def layer1(t, m):
                    base[:] = [t * STEPS1 + STEPS0 * NB, 0]
                    thr, n_ge, n_gt, need = (col[0:m, i:i + 1] for i in range(8, 12))
                    cand, bit, mask = (icol[0:m, i:i + 1] for i in range(3))
                    dve.wait_ge(s_tanh, t * 2 + 2)
                    done(dve.scalar_tensor_tensor(weights[0:m, :], a_rows[0:m, :], 0.0, weights[0:m, :],
                                                  ALU.is_gt, ALU.mult))
                    done(dve.memset(thr, 0.0))
                    done(dve.memset(bit, 1 << TOP_BIT))
                    dve.sem_inc(s_passed, 1)
                    start = base[0] + base[1]
                    with dve.Fori(0, TOP_BIT + 1) as i:
                        base[:] = [start + i * PER_BIT, 0]
                        done(dve.tensor_tensor(cand, thr.bitcast(I32), bit, ALU.bitwise_or))
                        done(dve.tensor_scalar(scratch[0:m, :], weights[0:m, :], cand.bitcast(F32), None,
                                               ALU.is_ge, ALU.add, accum_out=n_ge))
                        done(dve.tensor_scalar(mask, n_ge, float(TOPK), None, ALU.is_ge))
                        dve.sem_inc(s_passed, 1)
                        done(dve.copy_predicated(thr.bitcast(I32), mask, cand))
                        done(dve.tensor_scalar(bit, bit, 1, None, ALU.logical_shift_right))
                        assert base[1] == PER_BIT
                    base[:] = [start + PER_BIT * (TOP_BIT + 1), 0]
                    done(dve.tensor_scalar(scratch[0:m, :], weights[0:m, :], thr, None,
                                           ALU.is_gt, ALU.add, accum_out=n_gt))
                    done(dve.tensor_scalar(need, n_gt, -1.0, float(TOPK), ALU.mult, ALU.add))
                    done(dve.tensor_scalar(scratch[0:m, :], weights[0:m, :], thr, None, ALU.is_equal))
                    done(dve.tensor_tensor_scan(a_rows[0:m, :], scratch[0:m, :], scratch[0:m, :], 0.0,
                                                ALU.add, ALU.max))
                    done(dve.scalar_tensor_tensor(scratch[0:m, :], a_rows[0:m, :], need, scratch[0:m, :],
                                                  ALU.is_le, ALU.mult))
                    dve.sem_inc(s_rows_free, 1)
                    done(dve.scalar_tensor_tensor(scratch[0:m, :], weights[0:m, :], thr, scratch[0:m, :],
                                                  ALU.is_gt, ALU.add))
                    done(dve.tensor_tensor(weights[0:m, :], weights[0:m, :], scratch[0:m, :], ALU.mult))
                    dve.sem_inc(s_scaled, 1)
                    dve.wait_ge(s_support, t + (NB + 1))
                    done(dve.tensor_tensor(z1[0:m, :], support[0:m, :], bg_all[0:m, :], ALU.add))
                    done(dve.scalar_tensor_tensor(z[0:m, :], z1[0:m, :], 0.0, at(x1, t, m),
                                                  ALU.max, ALU.add))
                    dve.wait_ge(s_out, t * 16 + 16)
                    layer_norm(t + NB, m, z, result).then_inc(s_result, 1)
                    assert start is not None and base[1] == STEPS1 - 3 - PER_BIT * (TOP_BIT + 1)

                with dve.Fori(0, FULL) as t:
                    layer0(t, P)
                layer0(FULL, TAIL)
                with dve.Fori(0, FULL) as t:
                    layer1(t, P)
                layer1(FULL, TAIL)



def gnn_kernel(nc, x, adj, h0, y, w_proj, b_proj, w_gcn, b_gcn, out):
    with nc.sbuf_tensor("flag", [1, 1], I32) as flag:
        packed_path(nc, x, adj, h0, y, w_proj, b_proj, w_gcn, b_gcn, out, flag)
        general_path(nc, x, adj, h0, y, w_proj, b_proj, w_gcn, b_gcn, out, flag)


_INS = ['x', 'adj', 'L0_gnn_h0', 'L0_gnn_y', 'L1_gnn_W_proj', 'L1_gnn_b_proj', 'L1_gnn_W_gcn', 'L1_gnn_b_gcn']


def kernel(**inputs):
    import numpy as _np
    import concourse.bacc as _bacc
    from concourse import mybir as _mybir
    from concourse.bass_utils import run_bass_kernel_spmd as _run

    nc = _bacc.Bacc("TRN2", target_bir_lowering=False, num_devices=1)
    arrays, args = {}, []
    for name in _INS:
        a = _np.ascontiguousarray(inputs[name])
        arrays[f"in_{name}_dram"] = a
        args.append(nc.dram_tensor(f"in_{name}_dram", a.shape, _mybir.dt.from_np(a.dtype), kind="ExternalInput").ap())
    shape = inputs['x'].shape
    args.append(nc.dram_tensor("out_0_dram", shape, _mybir.dt.from_np(_np.dtype('float32')), kind="ExternalOutput").ap())
    gnn_kernel(nc, *args)
    r = _run(nc, [arrays], core_ids=[0])
    return r.results[0]["out_0_dram"]
```
